# Optimizing a Trainium2 kernel written in Bass

```python
import numpy as np
import jax
import jax.numpy as jnp

def _softmax(x, axis=-1):
    return jax.nn.softmax(x, axis=axis)
def _gelu(x):
    return jax.nn.gelu(x, approximate=True)
def _silu(x):
    return jax.nn.silu(x)
def _sigmoid(x):
    return jax.nn.sigmoid(x)
def _layernorm(x, axis=-1, eps=1e-5):
    m = jnp.mean(x, axis=axis, keepdims=True)
    v = jnp.var(x, axis=axis, keepdims=True)
    return (x - m) / jnp.sqrt(v + eps)
def _scatter_add(tgt, idx, src, axis=0):
    return tgt.at[idx].add(src)
def _segment_sum(src, seg, n):
    return jax.ops.segment_sum(src, seg, n)

kernel_name = 'mk_conv_seq_d2_conv_nhwc96_71f6a7'

def setup_inputs(seed: int = 0):
    np.random.seed(seed)
    _w = jnp.asarray
    def _rec_inputs():
        import jax
        import jax.numpy as jnp
        _gk = jax.random.key(seed)
        x = 1.648e-05 + 1 * jax.random.normal(jax.random.fold_in(_gk, 1), (8, 128, 96, 96), jnp.float32)
        return x
    x = _rec_inputs()
    def _L0_conv_setup():
        import jax, jax.numpy as jnp
        import numpy as np
        KS = 3

        def conv1x1(x, w, b=None):
            y = jnp.einsum('nchw,oc->nohw', x, w)
            if b is not None:
                y = y + b[None, :, None, None]
            return y

        def unfold3(x, d):
            N, C, H, W = x.shape
            xp = jnp.pad(x, ((0, 0), (0, 0), (d, d), (d, d)))
            cols = [xp[:, :, i * d:i * d + H, j * d:j * d + W] for i in range(KS) for j in range(KS)]
            return jnp.stack(cols, axis=2)

        def neighborhoods(feat):
            u1 = unfold3(feat, 1)
            u3 = unfold3(feat, 3)
            u3 = jnp.concatenate([u3[:, :, :4], u3[:, :, 5:]], axis=2)
            return jnp.concatenate([u1, u3], axis=2)
        key = jax.random.key(seed)
        ks = jax.random.split(key, 16)
        F_, C, H, W = (8, 128, 96, 96)
        I = 64
        s = 0.05
        d = {'x': jax.random.normal(ks[0], (F_, C, H, W), jnp.float32), 'rgb': jax.random.normal(ks[1], (1, C, H, W), jnp.float32), 'g_w': jax.random.normal(ks[2], (I, C), jnp.float32) * s, 'g_b': jax.random.normal(ks[3], (I,), jnp.float32) * s, 'theta_w': jax.random.normal(ks[4], (I, C), jnp.float32) * s, 'theta_b': jax.random.normal(ks[5], (I,), jnp.float32) * s, 'phi_w': jax.random.normal(ks[6], (I, C), jnp.float32) * s, 'phi_b': jax.random.normal(ks[7], (I,), jnp.float32) * s, 'W_w': jax.random.normal(ks[8], (C, I), jnp.float32) * s, 'W_b': jax.random.normal(ks[9], (C,), jnp.float32) * s, 'rgb_g_w': jax.random.normal(ks[10], (I, C), jnp.float32) * s, 'rgb_g_b': jnp.zeros((I,), jnp.float32), 'rgb_theta_w': jax.random.normal(ks[11], (I, C), jnp.float32) * s, 'rgb_theta_b': jnp.zeros((I,), jnp.float32), 'rgb_phi_w': jax.random.normal(ks[12], (I, C), jnp.float32) * s, 'rgb_phi_b': jnp.zeros((I,), jnp.float32), 'rgb_W_w': jax.random.normal(ks[13], (C, I), jnp.float32) * s, 'rgb_W_b': jax.random.normal(ks[14], (C,), jnp.float32) * s, 'cp_w': jax.random.normal(ks[15], (2 * I,), jnp.float32) * s}
        return d
    _L0_conv_all = _L0_conv_setup()
    _L0_conv_in = {k: v for k, v in _L0_conv_all.items() if k in ('rgb', 'g_w', 'g_b', 'theta_w', 'theta_b', 'phi_w', 'phi_b', 'W_w', 'W_b', 'rgb_g_w', 'rgb_g_b', 'rgb_theta_w', 'rgb_theta_b', 'rgb_phi_w', 'rgb_phi_b', 'rgb_W_w', 'rgb_W_b', 'cp_w', )}
    del _L0_conv_all

    def _L1_conv_setup():
        import jax, jax.numpy as jnp
        import numpy as np
        B, C, CI, H, W = (4, 128, 64, 96, 96)
        SS = 2
        BN_EPS = 1e-05

        def conv1x1(x, w, b):
            return jnp.einsum('bchw,oc->bohw', x, w) + b[None, :, None, None]

        def maxpool2(x):
            b, c, h, w = x.shape
            return x.reshape(b, c, h // 2, 2, w // 2, 2).max(axis=(3, 5))
        key = jax.random.key(seed)
        ks = jax.random.split(key, 12)
        s_in = 1.0 / np.sqrt(C)
        s_ci = 1.0 / np.sqrt(CI)
        return {'x': jax.random.normal(ks[0], (B, C, H, W), jnp.float32), 'g_w': jax.random.normal(ks[1], (CI, C), jnp.float32) * s_in, 'g_b': jax.random.normal(ks[2], (CI,), jnp.float32) * 0.01, 'theta_w': jax.random.normal(ks[3], (CI, C), jnp.float32) * s_in, 'theta_b': jax.random.normal(ks[4], (CI,), jnp.float32) * 0.01, 'phi_w': jax.random.normal(ks[5], (CI, C), jnp.float32) * s_in, 'phi_b': jax.random.normal(ks[6], (CI,), jnp.float32) * 0.01, 'W_w': jax.random.normal(ks[7], (C, CI), jnp.float32) * s_ci, 'W_b': jax.random.normal(ks[8], (C,), jnp.float32) * 0.01, 'bn_gamma': jax.random.normal(ks[9], (C,), jnp.float32) * 0.1 + 1.0, 'bn_beta': jax.random.normal(ks[10], (C,), jnp.float32) * 0.1, 'bn_mean': jax.random.normal(ks[11], (C,), jnp.float32) * 0.1, 'bn_var': jax.random.uniform(jax.random.fold_in(key, 99), (C,), jnp.float32, 0.5, 1.5)}
    _L1_conv_all = _L1_conv_setup()
    _L1_conv_in = {k: v for k, v in _L1_conv_all.items() if k in ('g_w', 'g_b', 'theta_w', 'theta_b', 'phi_w', 'phi_b', 'W_w', 'W_b', 'bn_gamma', 'bn_beta', 'bn_mean', 'bn_var', )}
    del _L1_conv_all

    return {
        "x": x,
        "L0_conv_rgb": _L0_conv_in["rgb"],
        "L0_conv_g_w": _L0_conv_in["g_w"],
        "L0_conv_g_b": _L0_conv_in["g_b"],
        "L0_conv_theta_w": _L0_conv_in["theta_w"],
        "L0_conv_theta_b": _L0_conv_in["theta_b"],
        "L0_conv_phi_w": _L0_conv_in["phi_w"],
        "L0_conv_phi_b": _L0_conv_in["phi_b"],
        "L0_conv_W_w": _L0_conv_in["W_w"],
        "L0_conv_W_b": _L0_conv_in["W_b"],
        "L0_conv_rgb_g_w": _L0_conv_in["rgb_g_w"],
        "L0_conv_rgb_g_b": _L0_conv_in["rgb_g_b"],
        "L0_conv_rgb_theta_w": _L0_conv_in["rgb_theta_w"],
        "L0_conv_rgb_theta_b": _L0_conv_in["rgb_theta_b"],
        "L0_conv_rgb_phi_w": _L0_conv_in["rgb_phi_w"],
        "L0_conv_rgb_phi_b": _L0_conv_in["rgb_phi_b"],
        "L0_conv_rgb_W_w": _L0_conv_in["rgb_W_w"],
        "L0_conv_rgb_W_b": _L0_conv_in["rgb_W_b"],
        "L0_conv_cp_w": _L0_conv_in["cp_w"],
        "L1_conv_g_w": _L1_conv_in["g_w"],
        "L1_conv_g_b": _L1_conv_in["g_b"],
        "L1_conv_theta_w": _L1_conv_in["theta_w"],
        "L1_conv_theta_b": _L1_conv_in["theta_b"],
        "L1_conv_phi_w": _L1_conv_in["phi_w"],
        "L1_conv_phi_b": _L1_conv_in["phi_b"],
        "L1_conv_W_w": _L1_conv_in["W_w"],
        "L1_conv_W_b": _L1_conv_in["W_b"],
        "L1_conv_bn_gamma": _L1_conv_in["bn_gamma"],
        "L1_conv_bn_beta": _L1_conv_in["bn_beta"],
        "L1_conv_bn_mean": _L1_conv_in["bn_mean"],
        "L1_conv_bn_var": _L1_conv_in["bn_var"],
    }

def reference(x, L0_conv_rgb, L0_conv_g_w, L0_conv_g_b, L0_conv_theta_w, L0_conv_theta_b, L0_conv_phi_w, L0_conv_phi_b, L0_conv_W_w, L0_conv_W_b, L0_conv_rgb_g_w, L0_conv_rgb_g_b, L0_conv_rgb_theta_w, L0_conv_rgb_theta_b, L0_conv_rgb_phi_w, L0_conv_rgb_phi_b, L0_conv_rgb_W_w, L0_conv_rgb_W_b, L0_conv_cp_w, L1_conv_g_w, L1_conv_g_b, L1_conv_theta_w, L1_conv_theta_b, L1_conv_phi_w, L1_conv_phi_b, L1_conv_W_w, L1_conv_W_b, L1_conv_bn_gamma, L1_conv_bn_beta, L1_conv_bn_mean, L1_conv_bn_var):
    import jax
    import jax.numpy as jnp
    def _L0_conv_ref(x, rgb, g_w, g_b, theta_w, theta_b, phi_w, phi_b, W_w, W_b, rgb_g_w, rgb_g_b, rgb_theta_w, rgb_theta_b, rgb_phi_w, rgb_phi_b, rgb_W_w, rgb_W_b, cp_w):
        import jax, jax.numpy as jnp
        import numpy as np
        KS = 3

        def conv1x1(x, w, b=None):
            y = jnp.einsum('nchw,oc->nohw', x, w)
            if b is not None:
                y = y + b[None, :, None, None]
            return y

        def unfold3(x, d):
            N, C, H, W = x.shape
            xp = jnp.pad(x, ((0, 0), (0, 0), (d, d), (d, d)))
            cols = [xp[:, :, i * d:i * d + H, j * d:j * d + W] for i in range(KS) for j in range(KS)]
            return jnp.stack(cols, axis=2)

        def neighborhoods(feat):
            u1 = unfold3(feat, 1)
            u3 = unfold3(feat, 3)
            u3 = jnp.concatenate([u3[:, :, :4], u3[:, :, 5:]], axis=2)
            return jnp.concatenate([u1, u3], axis=2)
        F_, C, H, W = x.shape
        P = H * W
        I = g_w.shape[0]
        T = 17
        g = neighborhoods(conv1x1(x, g_w, g_b)).reshape(F_, I, T, P)
        g = g.transpose(3, 0, 2, 1).reshape(P, F_ * T, I)
        th = neighborhoods(conv1x1(x, theta_w, theta_b)).reshape(F_, I, T, P)
        th = th.transpose(3, 1, 0, 2).reshape(P, I, F_ * T)
        ph = conv1x1(x, phi_w, phi_b).reshape(F_, I, P).transpose(2, 0, 1)
        f = jnp.einsum('pfc,pck->pfk', ph, th)
        attn = jax.nn.softmax(f, axis=-1)
        y = jnp.einsum('pfk,pkc->pfc', attn, g)
        y = y.transpose(1, 2, 0).reshape(F_, I, H, W)
        W_y = conv1x1(y, W_w, W_b)
        g_r = neighborhoods(conv1x1(rgb, rgb_g_w, rgb_g_b)).reshape(1, I, T, P)[0]
        g_r = g_r.transpose(2, 1, 0)
        th_r = neighborhoods(conv1x1(rgb, rgb_theta_w, rgb_theta_b)).reshape(1, I, T, P)[0]
        ph_r = conv1x1(x, rgb_phi_w, rgb_phi_b).reshape(F_, I, P)
        wt, wp = (cp_w[:I], cp_w[I:])
        a = jnp.einsum('c,ctp->pt', wt, th_r)
        b = jnp.einsum('c,fcp->pf', wp, ph_r)
        f_r = jax.nn.relu(a[:, None, :] + b[:, :, None]) / T
        y_r = jnp.einsum('pft,pti->pfi', f_r, g_r)
        y_r = y_r.transpose(1, 2, 0).reshape(F_, I, H, W)
        W_y_r = conv1x1(y_r, rgb_W_w, rgb_W_b)
        return W_y + W_y_r + x

    def _L1_conv_ref(x, g_w, g_b, theta_w, theta_b, phi_w, phi_b, W_w, W_b, bn_gamma, bn_beta, bn_mean, bn_var):
        import jax, jax.numpy as jnp
        import numpy as np
        B, C, CI, H, W = (4, 128, 64, 96, 96)
        SS = 2
        BN_EPS = 1e-05

        def conv1x1(x, w, b):
            return jnp.einsum('bchw,oc->bohw', x, w) + b[None, :, None, None]

        def maxpool2(x):
            b, c, h, w = x.shape
            return x.reshape(b, c, h // 2, 2, w // 2, 2).max(axis=(3, 5))
        b = x.shape[0]
        g_x = maxpool2(conv1x1(x, g_w, g_b)).reshape(b, CI, -1).transpose(0, 2, 1)
        theta_x = conv1x1(x, theta_w, theta_b).reshape(b, CI, -1).transpose(0, 2, 1)
        phi_x = maxpool2(conv1x1(x, phi_w, phi_b)).reshape(b, CI, -1)
        f = jnp.einsum('bqc,bck->bqk', theta_x, phi_x)
        attn = jax.nn.softmax(f, axis=-1)
        y = jnp.einsum('bqk,bkc->bqc', attn, g_x)
        y = y.transpose(0, 2, 1).reshape(b, CI, H, W)
        W_y = conv1x1(y, W_w, W_b)
        inv = bn_gamma * jax.lax.rsqrt(bn_var + BN_EPS)
        W_y = W_y * inv[None, :, None, None] + (bn_beta - bn_mean * inv)[None, :, None, None]
        return W_y + x

    def _gn(v, G=32, eps=1e-5):
        B_, H_, W_, C_ = v.shape
        g = v.reshape(B_, H_, W_, G, C_ // G)
        m = jnp.mean(g, axis=(1, 2, 4), keepdims=True)
        s = jnp.var(g, axis=(1, 2, 4), keepdims=True)
        return ((g - m) / jnp.sqrt(s + eps)).reshape(v.shape)

    def _ln_c(v, eps=1e-6):
        m = jnp.mean(v, axis=-1, keepdims=True)
        s = jnp.var(v, axis=-1, keepdims=True)
        return (v - m) / jnp.sqrt(s + eps)

    def _ln_t(v, eps=1e-5):
        m = jnp.mean(v, axis=-1, keepdims=True)
        s = jnp.var(v, axis=-1, keepdims=True)
        return (v - m) / jnp.sqrt(s + eps)

    def _to_tokens(v):
        B_, H_, W_, C_ = v.shape
        return v.reshape(B_, H_ * W_, C_)
    def _from_tokens(t, like):
        return t.reshape(like.shape)

    x = _L0_conv_ref(x, L0_conv_rgb, L0_conv_g_w, L0_conv_g_b, L0_conv_theta_w, L0_conv_theta_b, L0_conv_phi_w, L0_conv_phi_b, L0_conv_W_w, L0_conv_W_b, L0_conv_rgb_g_w, L0_conv_rgb_g_b, L0_conv_rgb_theta_w, L0_conv_rgb_theta_b, L0_conv_rgb_phi_w, L0_conv_rgb_phi_b, L0_conv_rgb_W_w, L0_conv_rgb_W_b, L0_conv_cp_w)
    x = _L1_conv_ref(x, L1_conv_g_w, L1_conv_g_b, L1_conv_theta_w, L1_conv_theta_b, L1_conv_phi_w, L1_conv_phi_b, L1_conv_W_w, L1_conv_W_b, L1_conv_bn_gamma, L1_conv_bn_beta, L1_conv_bn_mean, L1_conv_bn_var)
    return x


_drawn_inputs = setup_inputs


def setup_inputs(seed=0):
    import zlib

    import numpy as np

    out = dict(_drawn_inputs(seed))
    spreads = {'L0_conv_rgb_g_b': (0.0, 0.8),
     'L0_conv_rgb_theta_b': (0.0, 0.8),
     'L0_conv_rgb_phi_b': (0.0, 0.8)}
    factors = {'L0_conv_rgb': 3.092,
     'L0_conv_theta_b': 56.016,
     'L0_conv_rgb_g_w': 3.041,
     'L0_conv_rgb_theta_w': 4.7,
     'L0_conv_rgb_phi_w': 3.827,
     'L0_conv_rgb_W_w': 2.84,
     'L0_conv_cp_w': 3.72,
     'L1_conv_g_b': 64.0,
     'L1_conv_theta_b': 7.221,
     'L1_conv_phi_b': 64.0,
     'L1_conv_W_b': 64.0,
     'L1_conv_bn_beta': 8.0,
     'L1_conv_bn_mean': 8.0}
    for name, (base, spread) in spreads.items():
        noise = np.random.default_rng([zlib.crc32(name.encode()), seed]).standard_normal(out[name].shape)
        drawn = base * np.exp(spread * noise) if base else spread * noise
        out[name] = jnp.asarray(drawn.astype(out[name].dtype))
    for name, factor in factors.items():
        out[name] = (out[name] * factor).astype(out[name].dtype)
    return out
```

```python
from contextlib import ExitStack

import numpy as np

import concourse.bass as bass
from concourse import mybir

F32 = mybir.dt.float32
F32R = mybir.dt.float32r
ALU = mybir.AluOpType
ACT = mybir.ActivationFunctionType
AX = mybir.AxisListType

P = 128
CH, CI = 128, 64
HEIGHT = WIDTH = 96
POS = HEIGHT * WIDTH
FRAMES = 8
PW = WIDTH + 6
TILE_COLS = 16
TAPROWS = 5
TAPS = 17
RING = 8
QC = 512
UNROLL = 3


def column(vector):
    return vector.rearrange("(c one) -> c one", one=1)


def windows(row, width, count):
    k = row.shape[1]
    return bass.AP(row.tensor, row.offset, [[k, width], [TILE_COLS * k, count], [1, k]])


def row_windows(rows, width, count):
    part, frames, step = rows.ap
    return bass.AP(rows.tensor, rows.offset, [part, [TILE_COLS, count], frames, [1, width]])


def wait_apart(eng, passed, waits):
    waits = [(s, v if isinstance(v, int) else eng.snap(eng.to_reg(v))) for s, v in waits]
    eng.wait_ge(*passed)
    for s, v in waits:
        eng.wait_ge(s, v)


def rgb_fields(nc, rgb, g_w, g_b, theta_w, theta_b, cp_w, identity_dram, gr_dram, a_dram):
    ROWS = 8
    STEPS = HEIGHT // ROWS
    with ExitStack() as ctx:
        def sb(name, shape, dt=F32):
            return ctx.enter_context(nc.sbuf_tensor(name, shape, dt))

        def sem(name):
            return ctx.enter_context(nc.semaphore(name))

        x_sb = sb("rgb_sb", [P, 2, ROWS, WIDTH])
        zeros = sb("rgb_zeros", [PW, 3 * CI])
        ident = sb("rgb_ident", [P, P])
        g_nat = sb("rg_nat", [CI, CH])
        th_nat = sb("rth_nat", [CI, CH])
        vec = sb("rgb_vec", [CI, 2])
        g_bias = sb("rg_bias", [WIDTH, CI])
        w_g = sb("rw_g", [CH, CI])
        w_a = sb("rw_a", [CH, 1])
        b_a = sb("rb_a", [1, 1])
        g_sb = sb("rg_sb", [WIDTH, 2, ROWS, CI])
        a_sb = sb("ra_sb", [1, 2, ROWS, WIDTH])
        g_ps = ctx.enter_context(nc.psum_tensor("rg_ps", [P, 2, 512], F32))
        a_ps = ctx.enter_context(nc.psum_tensor("ra_ps", [P, 2, 512], F32))
        w_ps = ctx.enter_context(nc.psum_tensor("rw_ps", [P, 512], F32))

        consts = sem("r_consts")
        zeroed = sem("r_zeroed")
        padded = sem("r_padded")
        loaded = [sem(f"r_loaded{u}") for u in range(2)]
        prepared = sem("r_prepared")
        w_ready = sem("r_w_ready")
        g_done = sem("r_g_done")
        a_done = sem("r_a_done")
        g_ready = sem("r_g_ready")
        a_ready = sem("r_a_ready")
        g_stored = [sem(f"r_g_stored{u}") for u in range(2)]
        a_stored = [sem(f"r_a_stored{u}") for u in range(2)]

        block = ctx.enter_context(nc.Block())

        @block.sync
        def _(sp):
            sp.dma_start(ident[:, :], identity_dram).then_inc(consts, 16)
            sp.dma_start(g_nat[:, :], g_w).then_inc(consts, 16)
            sp.dma_start(th_nat[:, :], theta_w).then_inc(consts, 16)
            sp.dma_start(vec[:, 0:1], column(cp_w[0:CI])).then_inc(consts, 16)
            sp.dma_start(vec[:, 1:2], column(theta_b)).then_inc(consts, 16)
            sp.dma_start(g_bias[:, :], g_b.rearrange("(o c) -> o c", o=1).broadcast_to([WIDTH, CI])
                         ).then_inc(consts, 16)

            def load(step, u):
                sp.dma_start(x_sb[:, u, :, :], rgb[:, bass.ds(step * ROWS, ROWS), :]).then_inc(loaded[u], 16)

            def store(step, u):
                sp.wait_ge(g_ready, step + 2)
                sp.dma_start(gr_dram[bass.ds(step * ROWS + 3, ROWS), 3:3 + WIDTH, :].rearrange("r c k -> c r k"),
                             g_sb[:, u, :, :]).then_inc(g_stored[u], 16)
                sp.wait_ge(a_ready, step + 2)
                sp.dma_start(a_dram[bass.ds(step * ROWS + 3, ROWS), 3:3 + WIDTH].rearrange("(o r) c -> o r c", o=1),
                             a_sb[:, u, :, :]).then_inc(a_stored[u], 16)

            load(0, 0)
            load(1, 1)
            sp.wait_ge(zeroed, 1)
            for r0 in (0, 3 + HEIGHT):
                sp.dma_start(gr_dram[r0:r0 + 3, :, :].rearrange("r c k -> c r k"),
                             zeros[:, :].rearrange("c (r k) -> c r k", k=CI)).then_inc(padded, 16)
                sp.dma_start(a_dram[r0:r0 + 3, :], zeros[0:3, 0:PW]).then_inc(padded, 16)
            for c0 in (0, 3 + WIDTH):
                sp.dma_start(gr_dram[3:3 + HEIGHT, c0:c0 + 3, :], zeros[0:HEIGHT, :].rearrange("r (c k) -> r c k", k=CI)
                             ).then_inc(padded, 16)
                sp.dma_start(a_dram[3:3 + HEIGHT, c0:c0 + 3], zeros[0:HEIGHT, 0:3]).then_inc(padded, 16)
            with sp.Fori(0, STEPS // 2 - 1) as it:
                for u in range(2):
                    store(2 * it + u, u)
                    load(2 * it + 2 + u, u)
            for u in range(2):
                store(STEPS - 2 + u, u)
            sp.wait_ge(padded, 16 * 8)
            for u in range(2):
                sp.wait_ge(g_stored[u], 16 * (STEPS // 2 + 1))
                sp.wait_ge(a_stored[u], 16 * (STEPS // 2 + 1))

        @block.tensor
        def _(pe):
            pe.wait_ge(consts, 16 * 6)
            pe.transpose(w_ps[:, 0:CI], g_nat[:, :], ident[0:CI, 0:CI])
            pe.matmul(w_ps[:, CI:CI + 1], th_nat[:, :], vec[:, 0:1], start=True, stop=True)
            pe.matmul(w_ps[0:1, CI + 1:CI + 2], vec[:, 0:1], vec[:, 1:2], start=True, stop=True).then_inc(prepared, 1)
            pe.wait_ge(w_ready, 3)
            with pe.Fori(0, STEPS // 2) as it:
                for u in range(2):
                    pe.wait_ge(loaded[u], (it + 1) * 16)
                    pe.wait_ge(g_ready, it * 2 + (u + 1))
                    for r in range(ROWS):
                        mm = pe.matmul(g_ps[0:WIDTH, u, r * CI:(r + 1) * CI], x_sb[:, u, r, :], w_g[:, :],
                                       start=True, stop=True)
                    mm.then_inc(g_done, 1)
                    pe.wait_ge(a_ready, it * 2 + (u + 1))
                    for half in range(2):
                        mm = pe.matmul(a_ps[0:1, half, 0:4 * WIDTH], w_a[:, :], x_sb[:, u, 4 * half:4 * half + 4, :],
                                       start=True, stop=True)
                    mm.then_inc(a_done, 1)

        @block.scalar
        def _(act):
            act.sem_inc(a_ready, 1)
            for u in range(2):
                act.sem_inc(a_stored[u], 16)
            act.wait_ge(prepared, 1)
            act.copy(w_g[:, :], w_ps[:, 0:CI]).then_inc(w_ready, 1)
            act.copy(w_a[:, :], w_ps[:, CI:CI + 1]).then_inc(w_ready, 1)
            act.copy(b_a[:, :], w_ps[0:1, CI + 1:CI + 2]).then_inc(w_ready, 1)
            act.wait_ge(w_ready, 3)
            with act.Fori(0, STEPS // 2) as it:
                for u in range(2):
                    act.wait_ge(a_done, it * 2 + (u + 1))
                    act.wait_ge(a_stored[u], (it + 1) * 16)
                    act.activation(a_sb[:, u, :, :].rearrange("p (h r) c -> p h (r c)", h=2),
                                   a_ps[0:1, :, 0:4 * WIDTH], ACT.Identity, bias=b_a[:, :]).then_inc(a_ready, 1)

        @block.vector
        def _(dve):
            dve.memset(zeros[:, :], 0.0).then_inc(zeroed, 1)
            dve.sem_inc(g_ready, 1)
            for u in range(2):
                dve.sem_inc(g_stored[u], 16)
            dve.wait_ge(consts, 16 * 6)
            with dve.Fori(0, STEPS // 2) as it:
                for u in range(2):
                    dve.wait_ge(g_done, it * 2 + (u + 1))
                    dve.wait_ge(g_stored[u], (it + 1) * 16)
                    dve.tensor_tensor(g_sb[:, u, :, :], g_ps[0:WIDTH, u, :].rearrange("p (r k) -> p r k", k=CI),
                                      g_bias[:, :].rearrange("p (o k) -> p o k", o=1).broadcast_to([WIDTH, ROWS, CI]),
                                      ALU.add).then_inc(g_ready, 1)


def layer0(nc, x_dram, gr_dram, a_dram, x1_dram, identity_dram, mask_dram, rgb_mask_dram,
           g_w, g_b, theta_w, theta_b, phi_w, phi_b, W_w, W_b,
           rgb_phi_w, rgb_phi_b, rgb_W_w, rgb_W_b, cp_w):
    F = FRAMES
    WIN = TILE_COLS + 6
    TILES = WIDTH // TILE_COLS
    ROWKEYS = F * WIN
    NKEYS = TAPROWS * ROWKEYS
    HF = F // 2
    KB = HF * WIN
    BLOCKS = 2 * TAPROWS
    RK = TAPROWS * WIN
    LEAD = 4
    HALF = HF * WIDTH
    BIG = 3.0e38
    DY = (-3, -1, 0, 1, 3)
    UR = 4

    with ExitStack() as ctx:
        def sb(name, shape, dt=F32):
            return ctx.enter_context(nc.sbuf_tensor(name, shape, dt))

        def sem(name):
            return ctx.enter_context(nc.semaphore(name))

        ident = sb("ident0", [P, P])
        mask = sb("mask", [P, NKEYS])
        rgb_mask = sb("rgb_mask", [P, TAPROWS, WIN])
        nat = sb("nat", [P, 5, CH])
        vec = sb("vec", [CI, 2])
        cols = sb("cols0", [P, 5])
        B_TH, B_PH, B_OUT, B_OUT_R, B_B = (cols[:, n:n + 1] for n in range(5))
        w_th = sb("w_th", [P, P])
        w_ph = sb("w_ph", [P, CI + 1])
        w_g = sb("w_g0", [CH, CI])
        w_out = sb("w_out0", [P, CH])
        zeros = sb("zeros0", [P, 2 * CI])
        g_bias = sb("g_bias", [KB, TILES, 2, CI])

        th_hi = sb("th_hi", [P, RING, F, PW], F32R)
        th_lo = sb("th_lo", [CI, RING, F, PW], F32R)
        g_t = sb("g_t", [KB, RING, TILES, 2, CI])
        x_pad = sb("x_pad", [P, 2, F, PW])
        x_win = sb("x_win", [P, TILES, 2, KB])
        x_row = sb("x_row", [P, UR, F, WIDTH])
        ph_hl = sb("ph_hl", [P, 2, TILES, F, TILE_COLS], F32R)
        b_row = sb("b_row", [1, TILES, F, TILE_COLS])
        one = sb("one", [1, 1])
        b_col = sb("b_col", [P, 2, TILES])
        a_win = sb("a_win", [P, 2, TAPROWS, PW])
        gr_win = sb("gr_win", [RK, 2, TILES, CI])
        neg_s = sb("neg_s", [P, 2, NKEYS])
        neg_max = sb("neg_max0", [P, 2])
        probs = sb("probs0", [P, 2, NKEYS])
        sums = sb("sums", [P, TILES])
        factor = sb("factor", [P, TILES, 2])
        f_relu = sb("f_relu", [P, TAPROWS, WIN])
        f_rgb = sb("f_rgb", [P, 2, RK])
        p_t = sb("p_t", [RK, 2, BLOCKS + 1, P])
        y_sb = sb("y_sb0", [P, TILES, 2, CI])
        y_t = sb("y_t0", [P, 3 * P])
        z_row = sb("z_row", [P, 2, F, WIDTH])
        o_row = sb("o_row", [P, 2, F, WIDTH])

        s_ps = ctx.enter_context(nc.psum_tensor("s_ps", [P, 2, 512], F32))
        t_ps = ctx.enter_context(nc.psum_tensor("t_ps", [P, 3, 512], F32))
        y_ps = ctx.enter_context(nc.psum_tensor("y_ps", [P, 512], F32))
        ma_ps = ctx.enter_context(nc.psum_tensor("ma_ps", [P, 512], F32))
        mb_ps = ctx.enter_context(nc.psum_tensor("mb_ps", [P, 512], F32))

        consts = sem("consts0")
        biased = sem("biased0")
        patched = sem("patched0")
        zeroed = sem("zeroed0")
        th_zeroed = sem("th_zeroed")
        vecs_done = sem("vecs_done")
        w_turned = sem("w_turned0")
        w_ready = sem("w_ready0")
        pad_loaded = [sem(f"pad_loaded{u}") for u in range(2)]
        row_loaded = [sem(f"row_loaded{u}") for u in range(UR)]
        win_loaded = [sem(f"win_loaded{u}") for u in range(2)]
        win_copied = sem("win_copied")
        th_done = sem("th_done")
        th_high = sem("th_high")
        th_ready = sem("th_ready")
        g_done = sem("g_done")
        g_ready = sem("g_ready")
        ph_done = sem("ph_done")
        ph_high = sem("ph_high")
        ph_ready = sem("ph_ready")
        b_done = sem("b_done")
        b_ready = sem("b_ready")
        s_done = sem("s_done")
        s_masked = sem("s_masked")
        exp_done = sem("exp_done0")
        relu_done = sem("relu_done")
        f_ready = sem("f_ready")
        t_done = sem("t_done")
        t_act = sem("t_act")
        t_dve = sem("t_dve")
        pv_done = sem("pv_done0")
        inverted = sem("inverted0")
        y_ready = sem("y_ready0")
        yt_done = sem("yt_done0")
        yt_copied = sem("yt_copied0")
        z_done = sem("z_done0")
        z_ready = sem("z_ready0")
        o_ready = sem("o_ready")
        stored = [sem(f"stored0{u}") for u in range(2)]
        WIN_DMAS = 2 + TAPROWS
        NCONST = 19

        def rows_loop(eng, step):
            for u in range(UR):
                step(u, u, u, "first")
            with eng.Fori(1, HEIGHT // UR - 1) as it:
                for u in range(UR):
                    step(it * UR + u, u, None, "middle")
            for u in range(UR):
                r = HEIGHT - UR + u
                step(r, u, r, "last")

        block = ctx.enter_context(nc.Block())

        @block.sync
        def _(sp):
            def load_pad(t, par):
                sp.dma_start(x_pad[:, par, :, 3:3 + WIDTH],
                             x_dram[:, :, bass.ds(t, 1), :].rearrange("f c r w -> c f (r w)")).then_inc(pad_loaded[par], 16)

            def load_row(r, slot):
                sp.dma_start(x_row[:, slot, :, :],
                             x_dram[:, :, bass.ds(r, 1), :].rearrange("f c r w -> c f (r w)")).then_inc(row_loaded[slot], 16)

            def load_window(r, par):
                sp.dma_start(a_win[:, par, 0:3, :],
                             a_dram[bass.ds(r, 7), :].rearrange("(o r) c -> o r c", o=1)[:, 0:7:3, :]
                             .broadcast_to([P, 3, PW])).then_inc(win_loaded[par], 16)
                sp.dma_start(a_win[:, par, 3:5, :],
                             a_dram[bass.ds(r + 2, 3), :].rearrange("(o r) c -> o r c", o=1)[:, 0:3:2, :]
                             .broadcast_to([P, 2, PW])).then_inc(win_loaded[par], 16)
                for j, dy in enumerate((-3, 0, 3, -1, 1)):
                    src = gr_dram[bass.ds(r + 3 + dy, 1), :, :].rearrange("r c k -> (r c) k")
                    sp.dma_start(gr_win[j * WIN:(j + 1) * WIN, par, :, :], windows(src, WIN, TILES)
                                 ).then_inc(win_loaded[par], 16)

            sp.dma_start(ident[:, :], identity_dram).then_inc(consts, 16)
            for n, w in enumerate((theta_w, theta_w, phi_w, phi_w)):
                half = n % 2
                sp.dma_start(nat[half * CI:(half + 1) * CI, n // 2, :], w).then_inc(consts, 16)
            sp.dma_start(nat[0:CI, 2, :], g_w).then_inc(consts, 16)
            sp.dma_start(nat[0:CI, 4, :], rgb_phi_w).then_inc(consts, 16)
            sp.dma_start(nat[:, 3, 0:CI], W_w).then_inc(consts, 16)
            sp.dma_start(nat[:, 3, CI:CH], rgb_W_w).then_inc(consts, 16)
            sp.dma_start(vec[:, 0:1], column(cp_w[CI:2 * CI])).then_inc(consts, 16)
            sp.dma_start(vec[:, 1:2], column(rgb_phi_b)).then_inc(consts, 16)
            for half in range(2):
                sp.dma_start(B_TH[half * CI:(half + 1) * CI], column(theta_b)).then_inc(consts, 16)
                sp.dma_start(B_PH[half * CI:(half + 1) * CI], column(phi_b)).then_inc(consts, 16)
            sp.dma_start(B_OUT, column(W_b)).then_inc(consts, 16)
            sp.dma_start(B_OUT_R, column(rgb_W_b)).then_inc(consts, 16)
            sp.dma_start(mask[:, :], mask_dram).then_inc(consts, 16)
            sp.dma_start(rgb_mask[:, :, :], rgb_mask_dram.rearrange("p (r c) -> p r c", c=WIN)).then_inc(consts, 16)
            sp.dma_start(g_bias[:, :, :, :].rearrange("p t h k -> p (t h) k"),
                         g_b.rearrange("(o a c) -> o a c", o=1, a=1).broadcast_to([KB, 2 * TILES, CI])
                         ).then_inc(biased, 16)
            load_row(0, 0)
            load_row(1, 1)
            sp.wait_ge(biased, 16)
            sp.wait_ge(zeroed, 1)
            for f in range(HF):
                sp.dma_start(g_bias[f * WIN:f * WIN + 3, 0, :, :],
                             zeros[0:3, :].rearrange("p (h k) -> p h k", k=CI)).then_inc(patched, 16)
                sp.dma_start(g_bias[f * WIN + WIN - 3:(f + 1) * WIN, TILES - 1, :, :],
                             zeros[0:3, :].rearrange("p (h k) -> p h k", k=CI)).then_inc(patched, 16)
            sp.wait_ge(zeroed, 2)
            load_pad(0, 0)
            load_pad(1, 1)
            load_window(0, 0)
            for t in range(2, LEAD):
                sp.wait_ge(th_done, 2 * (t - 1))
                sp.wait_ge(win_copied, t - 1)
                load_pad(t, t % 2)

            def step(r, u, r_st, kind):
                if r_st is None or r_st + LEAD < HEIGHT:
                    sp.wait_ge(th_done, (r + (LEAD - 1)) * 2)
                    sp.wait_ge(win_copied, r + (LEAD - 1))
                    load_pad(r + LEAD, u % 2)
                if r_st is None or r_st >= 2:
                    sp.wait_ge(o_ready, r - 1 + 2)
                    sp.dma_start(x1_dram[:, :, bass.ds(r - 2, 1), :].rearrange("f c r w -> c f (r w)"),
                                 o_row[:, u % 2, :, :]).then_inc(stored[u % 2], 16)
                if r_st is None or r_st + 2 < HEIGHT:
                    load_row(r + 2, (u + 2) % UR)
                if r_st is None or r_st + 1 < HEIGHT:
                    if r_st != 0:
                        sp.wait_ge(pv_done, r * TILES)
                        sp.wait_ge(f_ready, r * TILES)
                    load_window(r + 1, (u + 1) % 2)

            rows_loop(sp, step)
            for r in (HEIGHT, HEIGHT + 1):
                sp.wait_ge(o_ready, r - 1 + 2)
                sp.dma_start(x1_dram[:, :, r - 2:r - 1, :].rearrange("f c r w -> c f (r w)"),
                             o_row[:, r % 2, :, :]).then_inc(stored[r % 2], 16)
            for u in range(2):
                sp.wait_ge(stored[u], 16 * (HEIGHT // 2 + 1))

        def slots(r, eng):
            return [(r + (dy + RING)) % RING for dy in DY]

        @block.tensor
        def _(pe):
            pe.wait_ge(consts, 16 * NCONST)
            pe.transpose(ma_ps[:, 0:P], nat[:, 0, :], ident[:, :]).then_inc(w_turned, 1)
            pe.transpose(ma_ps[:, P:2 * P], nat[:, 1, :], ident[:, :]).then_inc(w_turned, 1)
            pe.transpose(ma_ps[:, 2 * P:2 * P + CI], nat[0:CI, 2, :], ident[0:CI, 0:CI]).then_inc(w_turned, 1)
            pe.transpose(ma_ps[:, 3 * P:4 * P], nat[:, 3, :], ident[:, :]).then_inc(w_turned, 1)
            pe.matmul(mb_ps[:, 0:1], nat[0:CI, 4, :], vec[:, 0:1], start=True, stop=True)
            pe.matmul(mb_ps[:, 1:2], vec[:, 1:2].broadcast_to([CI, P]), vec[:, 0:1], start=True, stop=True
                      ).then_inc(vecs_done, 1)
            pe.wait_ge(w_ready, 8)

            def conv_th(h, par):
                pe.matmul(mb_ps[:, 0:HALF], w_th[:, :], x_pad[:, par, h * HF:(h + 1) * HF, 3:3 + WIDTH],
                          start=True, stop=True).then_inc(th_done, 1)

            def conv_g(h):
                for n in range(6):
                    ct, hf = 3 * h + n // 2, n % 2
                    mm = pe.matmul(mb_ps[0:KB, n * CI:(n + 1) * CI],
                                   x_win[:, ct, hf, :],
                                   w_g[:, :], start=True, stop=True)
                mm.then_inc(g_done, 1)

            def conv_ph(h, slot, bank):
                pe.matmul(bank[0:CI + 1, 0:HALF], w_ph[:, :], x_row[:, slot, h * HF:(h + 1) * HF, :],
                          start=True, stop=True).then_inc(ph_done, 1)

            def turn_b():
                for ct in range(TILES):
                    mm = pe.matmul(ma_ps[:, ct:ct + 1], b_row[:, ct, :, :].rearrange("p f c -> p (f c)"),
                                   one[:, :], start=True, stop=True)
                mm.then_inc(b_done, 1)

            for t in range(LEAD):
                pe.wait_ge(pad_loaded[t % 2], 16 * (t // 2 + 1))
                for h in range(2):
                    if t + h > 0:
                        pe.wait_ge(g_ready if h == 0 else th_ready, 2 * t + h)
                    conv_th(h, t % 2)
                pe.wait_ge(win_copied, t + 1)
                for h in range(2):
                    pe.wait_ge(th_ready if h == 0 else g_ready, 2 * t + (2 if h == 0 else 1))
                    conv_g(h)
            pe.wait_ge(row_loaded[0], 16)
            conv_ph(0, 0, ma_ps)
            pe.wait_ge(g_ready, 2 * LEAD)
            conv_ph(1, 0, mb_ps)
            pe.wait_ge(ph_ready, 2)
            turn_b()

            def scores(ct, par, sl):
                q = ph_hl[:, par, ct, :, :].rearrange("p f c -> p (f c)")
                q_hi = ph_hl[0:CI, par, ct, :, :].rearrange("p f c -> p (f c)")
                c0 = ct * TILE_COLS
                pieces = [(0, 0, 0, F), (0, ROWKEYS, 1, F), (0, 2 * ROWKEYS, 2, HF)]
                pieces += [(1, 0, 2, -HF), (1, KB, 3, F), (1, KB + ROWKEYS, 4, F)]
                for bank, at, j, nf in pieces:
                    f0, n = (HF, HF) if nf < 0 else (0, nf)
                    o = s_ps[:, bank, at:at + n * WIN]
                    pe.matmul(o, q, th_hi[:, bass.ds(sl[j], 1), f0:f0 + n, c0:c0 + WIN]
                              .rearrange("p a f c -> p (a f) c"), start=True, stop=False)
                    mm = pe.matmul(o, q_hi, th_lo[:, bass.ds(sl[j], 1), f0:f0 + n, c0:c0 + WIN]
                                   .rearrange("p a f c -> p (a f) c"), start=False, stop=True)
                mm.then_inc(s_done, 1)

            def turn_probs(par):
                for k in range(BLOCKS):
                    mm = pe.transpose(t_ps[0:KB, k // 4, (k % 4) * P:(k % 4 + 1) * P],
                                      probs[:, par, k * KB:(k + 1) * KB], ident[:, :])
                    if k == 3 or k == 7:
                        mm.then_inc(t_done, 1)
                pe.transpose(t_ps[0:RK, 2, 2 * P:3 * P], f_rgb[:, par, :], ident[:, :]).then_inc(t_done, 1)

            def values(ct, par, sl, wpar):
                for k in range(BLOCKS):
                    pe.matmul(y_ps[:, 0:CI], p_t[0:KB, par, k, :],
                              g_t[:, bass.ds(sl[k // 2], 1), ct, k % 2, :].rearrange("p a k -> p (a k)"),
                              start=(k == 0), stop=(k == BLOCKS - 1), skip_group_check=True)
                pe.matmul(y_ps[:, CI:2 * CI], p_t[0:RK, par, BLOCKS, :], gr_win[:, wpar, ct, :],
                          start=False, stop=True, skip_group_check=True).then_inc(pv_done, 1)

            def turn_y(h):
                for n in range(3):
                    mm = pe.transpose(ma_ps[:, n * P:(n + 1) * P],
                                      y_sb[:, 3 * h + n, :, :].rearrange("p a k -> p (a k)"), ident[:, :])
                mm.then_inc(yt_done, 1)

            def conv_out():
                pe.matmul(ma_ps[:, 0:3 * P], w_out[:, :], y_t[:, :], start=True, stop=True).then_inc(z_done, 1)

            def job_a(r, ct, u, r_st):
                back = r_st != 0
                ahead = r_st != HEIGHT - 1
                if ct == 0 and back:
                    pe.wait_ge(b_ready, r + 1)
                    pe.wait_ge(y_ready, (r - 1) * TILES + 3)
                    turn_y(0)
                if ct == 1 and back:
                    pe.wait_ge(yt_copied, r * 2 - 1)
                    conv_out()
                if ct == 2 and ahead:
                    if back:
                        pe.wait_ge(z_ready, r * 2 - 1)
                    else:
                        pe.wait_ge(b_ready, 1)
                    pe.wait_ge(row_loaded[(u + 1) % UR], rows_seen(r, u, r_st))
                    conv_ph(0, (u + 1) % UR, ma_ps)
                if ct == 3 and back:
                    if ahead:
                        pe.wait_ge(ph_ready, r * 2 + 3)
                    else:
                        pe.wait_ge(z_ready, r * 2 - 1)
                    pe.wait_ge(y_ready, r * TILES)
                    turn_y(1)
                if ct == 4 and back:
                    pe.wait_ge(yt_copied, r * 2)
                    conv_out()
                if ct == 5 and ahead:
                    if back:
                        pe.wait_ge(z_ready, r * 2)
                    pe.wait_ge(ph_ready, r * 2 + 4)
                    turn_b()

            def rows_seen(r, u, r_st):
                if r_st is not None:
                    return 16 * ((r_st + 1) // UR + 1)
                return (r - u) * (16 // UR) + 16 * (1 + (u + 1) // UR)

            def pads_seen(r, u, r_st):
                if r_st is not None:
                    return 16 * ((r_st + LEAD) // 2 + 1)
                return (r - u) * 8 + 16 * ((u + LEAD) // 2 + 1)

            def wins_seen(r, u, r_st, back=0):
                if r_st is not None:
                    return 16 * WIN_DMAS * ((r_st - back) // 2 + 1)
                return (r - u) * (8 * WIN_DMAS) + 16 * WIN_DMAS * ((u - back) // 2 + 1)

            def job_b(r, ct, u, r_st):
                more = r_st is None or r_st + LEAD < HEIGHT
                if more and ct == 0:
                    pe.wait_ge(ph_ready, r * 2 + 2)
                    pe.wait_ge(pad_loaded[u % 2], pads_seen(r, u, r_st))
                    conv_th(0, u % 2)
                if more and ct == 1:
                    pe.wait_ge(th_ready, (r + LEAD) * 2 + 1)
                    conv_th(1, u % 2)
                if more and ct == 2:
                    pe.wait_ge(th_ready, (r + LEAD) * 2 + 2)
                    pe.wait_ge(win_copied, r + (LEAD + 1))
                    conv_g(0)
                if more and ct == 3:
                    pe.wait_ge(g_ready, (r + LEAD) * 2 + 1)
                    conv_g(1)
                if ct == 4 and r_st != HEIGHT - 1:
                    if more:
                        pe.wait_ge(g_ready, (r + LEAD) * 2 + 2)
                    else:
                        pe.wait_ge(ph_ready, r * 2 + 2)
                    conv_ph(1, (u + 1) % UR, mb_ps)

            def step(r, u, r_st, kind):
                sl = slots(r, pe)
                before = slots(r - 1, pe) if r_st != 0 else None
                for ct in range(TILES):
                    n = r * TILES + ct
                    n_st = None if r_st is None else r_st * TILES + ct
                    par = ct % 2
                    if ct == 0:
                        pe.wait_ge(th_ready, (r + LEAD) * 2)
                        pe.wait_ge(ph_ready, r * 2 + 2)
                    if n_st != 0:
                        pe.wait_ge(s_masked, n)
                    scores(ct, u % 2, sl)
                    job_a(r, ct, u, r_st)
                    if n_st != 0:
                        pe.wait_ge(exp_done, n)
                        pe.wait_ge(f_ready, n)
                        if n_st != 1:
                            pe.wait_ge(t_act, n - 1)
                            pe.wait_ge(t_dve, n - 1)
                        turn_probs(1 - par)
                    job_b(r, ct, u, r_st)
                    if n_st is None or n_st >= 2:
                        if n_st != 2:
                            pe.wait_ge(y_ready, n - 2)
                        if ct == 2:
                            pe.wait_ge(g_ready, (r + LEAD) * 2)
                            pe.wait_ge(win_loaded[u % 2], wins_seen(r, u, r_st))
                        if ct >= 2:
                            values(ct - 2, par, sl, u % 2)
                        else:
                            values(ct + TILES - 2, par, before, (u + 1) % 2)

            rows_loop(pe, step)
            n = HEIGHT * TILES
            pe.wait_ge(exp_done, n)
            pe.wait_ge(f_ready, n)
            pe.wait_ge(t_act, n - 1)
            pe.wait_ge(t_dve, n - 1)
            turn_probs(1)
            pe.wait_ge(y_ready, n - 2)
            last = slots(HEIGHT - 1, pe)
            values(TILES - 2, 0, last, 1)
            pe.wait_ge(t_act, n)
            pe.wait_ge(t_dve, n)
            pe.wait_ge(y_ready, n - 1)
            values(TILES - 1, 1, last, 1)
            pe.wait_ge(z_ready, 2 * HEIGHT - 2)
            turn_y(0)
            pe.wait_ge(yt_copied, 2 * HEIGHT - 1)
            conv_out()
            pe.wait_ge(z_ready, 2 * HEIGHT - 1)
            pe.wait_ge(y_ready, n)
            turn_y(1)
            pe.wait_ge(yt_copied, 2 * HEIGHT)
            conv_out()

        @block.scalar
        def _(act):
            act.wait_ge(w_turned, 4)
            act.copy(w_th[:, :], ma_ps[:, 0:P]).then_inc(w_ready, 1)
            act.copy(w_ph[:, 0:CI], ma_ps[:, P:P + CI]).then_inc(w_ready, 1)
            act.copy(w_g[:, :], ma_ps[:, 2 * P:2 * P + CI]).then_inc(w_ready, 1)
            act.copy(w_out[0:CI, :], ma_ps[0:CI, 3 * P:4 * P]).then_inc(w_ready, 1)
            act.mul(w_out[CI:P, :], ma_ps[CI:P, 3 * P:4 * P], 1.0 / TAPS).then_inc(w_ready, 1)
            act.wait_ge(vecs_done, 1)
            act.copy(w_ph[:, CI:CI + 1], mb_ps[:, 0:1]).then_inc(w_ready, 1)
            act.copy(B_B, mb_ps[:, 1:2]).then_inc(w_ready, 1)
            act.wait_ge(w_ready, 8)
            act.wait_ge(th_zeroed, 1)

            def take_th(h, slot, count):
                act.wait_ge(th_done, count)
                act.activation(th_hi[:, bass.ds(slot, 1), h * HF:(h + 1) * HF, 3:3 + WIDTH]
                               .rearrange("p a f c -> p (a f) c"),
                               mb_ps[:, 0:HALF].rearrange("p (f c) -> p f c", c=WIDTH),
                               ACT.Identity, bias=B_TH).then_inc(th_high, 1)

            def take_ph(h, par, bank, count):
                act.wait_ge(ph_done, count)
                act.activation(ph_hl[0:CI, par, :, h * HF:(h + 1) * HF, :].rearrange("p t f c -> p f t c"),
                               bank[0:CI, 0:HALF].rearrange("p (f t c) -> p f t c", f=HF, c=TILE_COLS),
                               ACT.Identity, bias=B_PH[0:CI])
                act.copy(b_row[:, :, h * HF:(h + 1) * HF, :].rearrange("p t f c -> p f t c"),
                         bank[CI:CI + 1, 0:HALF].rearrange("p (f t c) -> p f t c", f=HF, c=TILE_COLS)
                         ).then_inc(ph_high, 1)

            def take_b(par, count):
                act.wait_ge(b_done, count)
                act.activation(b_col[:, par, :], ma_ps[:, 0:TILES], ACT.Identity, bias=B_B).then_inc(b_ready, 1)

            for t in range(LEAD):
                for h in range(2):
                    take_th(h, t, 2 * t + h + 1)
            for h, bank in enumerate((ma_ps, mb_ps)):
                take_ph(h, 0, bank, h + 1)
            take_b(0, 1)

            def exp(par, ct, n):
                act.wait_ge(s_masked, n + 1)
                act.activation(probs[:, par, :], neg_s[:, par, :], ACT.Exp, bias=neg_max[:, par:par + 1],
                               scale=-1.0, accum_out=sums[:, ct:ct + 1]).then_inc(exp_done, 1)

            def take_t(par, count):
                act.wait_ge(t_done, count)
                act.copy(p_t[0:KB, par, 0:4, :], t_ps[0:KB, 0, :].rearrange("p (k q) -> p k q", q=P)).then_inc(t_act, 1)

            def take_yt(count):
                act.wait_ge(yt_done, count)
                act.copy(y_t[:, :], ma_ps[:, 0:3 * P]).then_inc(yt_copied, 1)

            def take_z(h, par, count, row):
                act.wait_ge(z_done, count)
                act.wait_ge(o_ready, row + 1)
                act.activation(z_row[:, par, :, h * 3 * TILE_COLS:(h + 1) * 3 * TILE_COLS]
                               .rearrange("p f (t c) -> p t f c", c=TILE_COLS),
                               ma_ps[:, 0:3 * P].rearrange("p (t f c) -> p t f c", f=F, c=TILE_COLS),
                               ACT.Identity, bias=B_OUT).then_inc(z_ready, 1)

            def step(r, u, r_st, kind):
                slot = (r + LEAD) % RING
                back, ahead = r_st != 0, r_st != HEIGHT - 1
                more = r_st is None or r_st + LEAD < HEIGHT
                for ct in range(TILES):
                    n = r * TILES + ct
                    if ct in (0, 3) and back:
                        take_yt(r * 2 - 1 + ct // 3)
                    if ct in (1, 4) and back:
                        take_z(ct // 3, (u + 1) % 2, r * 2 - 1 + ct // 3, r - 1)
                    if ct == 2 and ahead:
                        take_ph(0, (u + 1) % 2, ma_ps, r * 2 + 3)
                    if ct == 5 and ahead:
                        take_b((u + 1) % 2, r + 2)
                    exp(ct % 2, ct, n)
                    if ct > 0 or r_st != 0:
                        take_t(1 - ct % 2, n * 3 - 2)
                    if ct < 2 and more:
                        take_th(ct, slot, (r + LEAD) * 2 + (ct + 1))
                    if ct == 4 and ahead:
                        take_ph(1, (u + 1) % 2, mb_ps, r * 2 + 4)

            rows_loop(act, step)
            take_t(1, HEIGHT * TILES * 3 - 2)
            for h in range(2):
                take_yt(2 * HEIGHT - 1 + h)
                take_z(h, 1, 2 * HEIGHT - 1 + h, HEIGHT - 1)

        @block.vector
        def _(dve):
            dve.memset(zeros[:, :], 0.0).then_inc(zeroed, 1)
            dve.memset(x_pad[:, :, :, :], 0.0).then_inc(zeroed, 1)
            dve.memset(th_lo[:, :, :, :].bitcast(F32), 0.0).then_inc(zeroed, 1)
            dve.memset(g_t[:, RING - 3:RING, :, :, :], 0.0).then_inc(zeroed, 1)
            dve.memset(one[:, :], 1.0)
            dve.memset(factor[:, :, :], 1.0).then_inc(zeroed, 1)
            dve.wait_ge(consts, 16 * NCONST)
            dve.tensor_tensor(B_OUT, B_OUT, B_OUT_R, ALU.add).then_inc(w_ready, 1)
            dve.wait_ge(zeroed, 5)
            dve.wait_ge(w_ready, 8)
            dve.wait_ge(patched, 16 * 2 * HF)

            def low_th(h, slot, count):
                dve.wait_ge(th_high, count)
                dve.scalar_tensor_tensor(th_lo[:, bass.ds(slot, 1), h * HF:(h + 1) * HF, 3:3 + WIDTH]
                                         .rearrange("p a f c -> p (a f) c"),
                                         mb_ps[0:CI, 0:HALF].rearrange("p (f c) -> p f c", c=WIDTH), B_TH[0:CI],
                                         th_hi[0:CI, bass.ds(slot, 1), h * HF:(h + 1) * HF, 3:3 + WIDTH]
                                         .rearrange("p a f c -> p (a f) c").bitcast(F32),
                                         ALU.add, ALU.subtract).then_inc(th_ready, 1)

            def take_g(h, slot, count):
                dve.wait_ge(g_done, count)
                dve.tensor_tensor(g_t[:, bass.ds(slot, 1), 3 * h:3 * h + 3, :, :].rearrange("p a t h k -> p (a t h k)"),
                                  mb_ps[0:KB, 0:6 * CI],
                                  g_bias[:, 3 * h:3 * h + 3, :, :].rearrange("p t h k -> p (t h k)"),
                                  ALU.add).then_inc(g_ready, 1)

            def low_ph(h, par, bank, count):
                dve.wait_ge(ph_high, count)
                for f in range(HF):
                    stt = dve.scalar_tensor_tensor(
                        ph_hl[CI:P, par, :, h * HF + f, :],
                        bank[0:CI, f * WIDTH:(f + 1) * WIDTH].rearrange("p (t c) -> p t c", c=TILE_COLS), B_PH[0:CI],
                        ph_hl[0:CI, par, :, h * HF + f, :].bitcast(F32), ALU.add, ALU.subtract)
                stt.then_inc(ph_ready, 1)

            for t in range(LEAD):
                for h in range(2):
                    low_th(h, t, 2 * t + h + 1)
                for h in range(2):
                    take_g(h, t, 2 * t + h + 1)
            for h, bank in enumerate((ma_ps, mb_ps)):
                low_ph(h, 0, bank, h + 1)

            def mask_scores(par, n):
                wait_apart(dve, (zeroed, 5), [(s_done, n + 1)])
                dve.tensor_tensor_reduce(neg_s[:, par, :].rearrange("p (b k) -> p b k", b=2), s_ps[:, :, 0:NKEYS // 2],
                                         mask[:, :].rearrange("p (b k) -> p b k", b=2), -1.0, BIG,
                                         ALU.add, ALU.min, neg_max[:, par:par + 1]).then_inc(s_masked, 1)

            def take_t(par, count):
                dve.wait_ge(t_done, count - 1)
                dve.tensor_copy(p_t[0:KB, par, 4:8, :], t_ps[0:KB, 1, :].rearrange("p (k q) -> p k q", q=P))
                dve.wait_ge(t_done, count)
                dve.tensor_copy(p_t[0:KB, par, 8:BLOCKS, :], t_ps[0:KB, 2, 0:2 * P].rearrange("p (k q) -> p k q", q=P))
                dve.tensor_copy(p_t[0:RK, par, BLOCKS, :], t_ps[0:RK, 2, 2 * P:3 * P]).then_inc(t_dve, 1)

            def divide(ct, n):
                dve.wait_ge(exp_done, n + 1)
                dve.reciprocal(factor[:, ct, 0:1], sums[:, ct:ct + 1]).then_inc(inverted, 1)
                dve.wait_ge(inverted, n + 1)
                dve.wait_ge(pv_done, n + 1)
                dve.tensor_tensor(y_sb[:, ct, :, :], y_ps[:, 0:2 * CI].rearrange("p (a k) -> p a k", k=CI),
                                  factor[:, ct, :].rearrange("p (a o) -> p a o", o=1).broadcast_to([P, 2, CI]),
                                  ALU.mult).then_inc(y_ready, 1)

            def step(r, u, r_st, kind):
                slot = (r + LEAD) % RING
                ahead = r_st != HEIGHT - 1
                more = r_st is None or r_st + LEAD < HEIGHT
                for ct in range(TILES):
                    n = r * TILES + ct
                    n_st = None if r_st is None else r_st * TILES + ct
                    mask_scores(ct % 2, n)
                    if ct == 2 and ahead:
                        low_ph(0, (u + 1) % 2, ma_ps, r * 2 + 3)
                    if n_st != 0:
                        take_t(1 - ct % 2, n * 3)
                    if ct < 2 and more:
                        low_th(ct, slot, (r + LEAD) * 2 + (ct + 1))
                    if ct in (2, 3) and more:
                        take_g(ct - 2, slot, (r + LEAD) * 2 + (ct - 1))
                    if ct == 4 and ahead:
                        low_ph(1, (u + 1) % 2, mb_ps, r * 2 + 4)
                    if n_st is None or n_st >= 2:
                        divide((ct - 2) % TILES, n - 2)
                    if ct == 2 and not more and ahead:
                        dve.memset(th_hi[:, slot, :, :].bitcast(F32), 0.0).then_inc(th_ready, 1)
                        dve.memset(th_lo[:, slot, :, :].bitcast(F32), 0.0).then_inc(th_ready, 1)
                        dve.memset(g_t[:, slot, :, :, :], 0.0).then_inc(g_ready, 2)

            rows_loop(dve, step)
            n = HEIGHT * TILES
            take_t(1, n * 3)
            divide(TILES - 2, n - 2)
            divide(TILES - 1, n - 1)

        @block.gpsimd
        def _(pool):
            pool.sem_inc(o_ready, 2)
            for u in range(2):
                pool.sem_inc(stored[u], 16)
            pool.memset(th_hi[:, :, :, :].bitcast(F32), 0.0).then_inc(th_zeroed, 1)
            pool.wait_ge(consts, 16 * NCONST)

            def rgb_weights(r, ct, u, r_st):
                n = r * TILES + ct
                n_st = None if r_st is None else r_st * TILES + ct
                waits = []
                if ct == 0:
                    waits.append((b_ready, r + 1))
                    waits.append((win_loaded[u % 2], (r - u) * (8 * WIN_DMAS) + 16 * WIN_DMAS * (u // 2 + 1)))
                if n_st != 0:
                    waits.append((f_ready, n))
                wait_apart(pool, (consts, 16 * NCONST), waits)
                pool.tensor_scalar(f_relu[:, :, :], a_win[:, u % 2, :, ct * TILE_COLS:ct * TILE_COLS + WIN],
                                   b_col[:, u % 2, ct:ct + 1], 0.0, ALU.add, ALU.max).then_inc(relu_done, 1)
                pool.wait_ge(relu_done, n + 1)
                if n_st is None or n_st >= 2:
                    pool.wait_ge(t_done, n * 3 - 3)
                pool.tensor_tensor(f_rgb[:, ct % 2, :].rearrange("p (r c) -> p r c", c=WIN), f_relu[:, :, :],
                                   rgb_mask[:, :, :], ALU.mult).then_inc(f_ready, 1)

            def copy_windows(par, t, seen):
                waits = [(pad_loaded[par], seen)]
                if not (isinstance(t, int) and t == 0):
                    waits.append((g_done, t * 2))
                wait_apart(pool, (consts, 16 * NCONST), waits)
                pool.tensor_copy(x_win[:, :, :, :].rearrange("p t h (f c) -> p t (h f) c", c=WIN),
                                 row_windows(x_pad[:, par, :, :], WIN, TILES)).then_inc(win_copied, 1)

            for t in range(LEAD):
                copy_windows(t % 2, t, 16 * (t // 2 + 1))

            def residual(slot, par, row, seen):
                pool.wait_ge(z_ready, row * 2 + 2)
                pool.wait_ge(stored[par], seen)
                pool.tensor_tensor(o_row[:, par, :, :], z_row[:, par, :, :], x_row[:, slot, :, :],
                                   ALU.add).then_inc(o_ready, 1)

            def step(r, u, r_st, kind):
                for ct in range(TILES):
                    rgb_weights(r, ct, u, r_st)
                    if ct == 0 and (r_st is None or r_st + LEAD < HEIGHT):
                        seen = (r - u) * 8 + 16 * ((u + LEAD) // 2 + 1)
                        copy_windows(u % 2, r + LEAD, seen)
                if r_st is None:
                    residual((u + 3) % UR, (u + 1) % 2, r - 1, (r - u) * 8 + 16 * ((u - 1) // 2 + 1))
                elif r_st > 0:
                    residual((u + 3) % UR, (u + 1) % 2, r - 1, 16 * ((r_st - 1) // 2 + 1))

            rows_loop(pool, step)
            residual(UR - 1, 1, HEIGHT - 1, 16 * ((HEIGHT - 1) // 2 + 1))


def layer1(nc, frames, x_dram, out_dram, g_w, g_b, theta_w, theta_b, phi_w, phi_b, W_w, W_b,
           bn_gamma, bn_beta, bn_mean, bn_var, identity_dram):
    CHUNKS = POS // QC
    GROUPS = CHUNKS // UNROLL
    KEYS = POS // 4
    KT = KEYS // P
    QT = QC // P
    CONV = 4 * WIDTH
    NCONV = POS // CONV
    SUB = 768
    SUBS = KEYS // SUB
    PARTS = QT * SUBS
    VW = CI + 1
    LAG = 2
    ROW_HI, ROW_LO = CI, CI + 32

    with ExitStack() as ctx:
        def sb(name, shape, dt=F32):
            return ctx.enter_context(nc.sbuf_tensor(name, shape, dt))

        def sem(name):
            return ctx.enter_context(nc.semaphore(name))

        x_sb = sb("x_sb", [P, 2, POS])
        w_nat = sb("w_nat", [P, 2, CH])
        wout_nat = sb("wout_nat", [P, CI])
        w_kv = sb("w_kv", [P, P])
        w_q = sb("w_q", [P, P])
        w_out = sb("w_out", [CI, CH])
        ident = sb("ident1", [P, P])
        cols = sb("cols", [P, 12])
        B_Q, B_PHI, B_G, B_W, GAMMA, BETA, MEAN, VAR, STD, INV, OFFSET, EPS = (
            cols[:, n:n + 1] for n in range(12))
        kv_raw = sb("kv_raw", [P, KEYS])
        v_f32 = sb("v_f32", [CI, KEYS])
        k_hi = sb("k_hi", [P, KEYS], F32R)
        k_lo = sb("k_lo", [P, KEYS], F32R)
        v_t = sb("v_t", [P, KT, VW])
        q_hl = sb("q_hl", [P, UNROLL, QC], F32R)
        q_mx = sb("q_mx", [P, UNROLL, QC], F32R)
        part_max = sb("part_max", [P, PARTS])
        neg_max = sb("neg_max", [P, QT])
        probs = sb("probs", [P, UNROLL, QC])
        o_sb = sb("o_sb", [P, QT * VW])
        o_rec = sb("o_rec", [P, QT])
        y_sb = sb("y_sb", [P, QT, CI])
        y_t = sb("y_t", [CI, QC])
        z_sb = sb("z_sb", [P, UNROLL, QC])
        res = sb("res", [P, UNROLL, QC])

        mx_ps = ctx.enter_context(nc.psum_tensor("mx_ps", [P, 4, 512], F32))
        st_ps = ctx.enter_context(nc.psum_tensor("st_ps", [P, 2, 512], F32))
        o_ps = ctx.enter_context(nc.psum_tensor("o_ps", [P, 512], F32))
        m_ps = ctx.enter_context(nc.psum_tensor("m_ps", [P, 512], F32))

        consts_loaded = sem("consts_loaded")
        zeroed = sem("zeroed")
        consts_ready = sem("consts_ready")
        std_ready = sem("std_ready")
        w_turned = sem("w_turned")
        w_ready = sem("w_ready")
        x_loaded = sem("x_loaded")
        kv_done = sem("kv_done")
        kv_pooled = sem("kv_pooled")
        khi_ready = sem("khi_ready")
        klo_ready = sem("klo_ready")
        v_biased = sem("v_biased")
        v_turned = sem("v_turned")
        v_ready = sem("v_ready")
        q_done = sem("q_done")
        q_copied = sem("q_copied")
        q_low = sem("q_low")
        mx_done = sem("mx_done")
        mx_reduced = sem("mx_reduced")
        max_ready = sem("max_ready")
        maxrow_done = sem("maxrow_done")
        maxrow_high = sem("maxrow_high")
        maxrow_low = sem("maxrow_low")
        st_done = sem("st_done")
        exp_done = sem("exp_done")
        pv_done = sem("pv_done")
        o_copied = sem("o_copied")
        o_inverted = sem("o_inverted")
        y_ready = sem("y_ready")
        yt_done = sem("yt_done")
        yt_copied = sem("yt_copied")
        z_done = sem("z_done")
        z_ready = sem("z_ready")
        res_ready = sem("res_ready")
        stored = [sem(f"stored{u}") for u in range(UNROLL)]

        XLOADS = 4
        PER = POS // XLOADS
        CREDIT = UNROLL

        def chunk_loop(eng, chunk):
            with eng.Fori(0, frames) as b:
                chunk.start(b)
                for u in range(UNROLL):
                    chunk(b, b * CHUNKS + u, u, u, u == 0, False)
                with eng.Fori(1, GROUPS - 1) as it:
                    for u in range(UNROLL):
                        chunk(b, b * CHUNKS + it * UNROLL + u, it * UNROLL + u, u, False, False)
                for u in range(UNROLL):
                    i = CHUNKS - UNROLL + u
                    chunk(b, b * CHUNKS + i, i, u, False, i)
                chunk.end(b)

        block = ctx.enter_context(nc.Block())

        @block.sync
        def _(sp):
            for n, w in enumerate((phi_w, g_w)):
                sp.dma_start(w_nat[n * CI:(n + 1) * CI, 0, :], w).then_inc(consts_loaded, 16)
                sp.dma_start(w_nat[n * CI:(n + 1) * CI, 1, :], theta_w).then_inc(consts_loaded, 16)
                sp.dma_start(B_Q[n * CI:(n + 1) * CI], column(theta_b)).then_inc(consts_loaded, 16)
            sp.dma_start(wout_nat[:, :], W_w).then_inc(consts_loaded, 16)
            sp.dma_start(ident[:, :], identity_dram).then_inc(consts_loaded, 16)
            sp.dma_start(B_PHI[0:CI], column(phi_b)).then_inc(consts_loaded, 16)
            sp.dma_start(B_G[CI:P], column(g_b)).then_inc(consts_loaded, 16)
            for dst, src in ((B_W, W_b), (GAMMA, bn_gamma), (BETA, bn_beta), (MEAN, bn_mean), (VAR, bn_var)):
                sp.dma_start(dst, column(src)).then_inc(consts_loaded, 16)

            def load(b, slot):
                for n in range(XLOADS):
                    sp.dma_start(x_sb[:, bass.ds(slot, 1), n * PER:(n + 1) * PER],
                                 x_dram[bass.ds(b, 1), :, n * PER:(n + 1) * PER].rearrange("a c n -> c a n")
                                 ).then_inc(x_loaded, 16)

            def stores(b):
                with sp.Fori(0, GROUPS) as it:
                    for u in range(UNROLL):
                        g = b * CHUNKS + it * UNROLL + u
                        sp.wait_ge(res_ready, g + 1 + CREDIT)
                        sp.dma_start(out_dram[bass.ds(b, 1), :, bass.ds(it * (UNROLL * QC) + u * QC, QC)]
                                     .rearrange("a c n -> c (a n)"), res[:, u, :]).then_inc(stored[u], 16)

            load(0, 0)
            sp.wait_ge(x_loaded, 16 * XLOADS)
            load(1, 1)
            if frames > 2:
                with sp.Fori(0, frames - 2) as b:
                    stores(b)
                    sp.wait_ge(res_ready, (b + 1) * CHUNKS + CREDIT)
                    sp.wait_ge(x_loaded, (b + 2) * (16 * XLOADS))
                    load(b + 2, b % 2)
            with sp.Fori(frames - 2, frames) as b:
                stores(b)
            for u in range(UNROLL):
                sp.wait_ge(stored[u], 16 * (frames * GROUPS + 1))

        @block.gpsimd
        def _(pool):
            pool.sem_inc(res_ready, CREDIT)
            for u in range(UNROLL):
                pool.sem_inc(stored[u], 16)
            with pool.Fori(0, frames) as b:
                with pool.Fori(0, GROUPS) as it:
                    for u in range(UNROLL):
                        g = b * CHUNKS + it * UNROLL + u
                        pool.wait_ge(z_ready, g + 2)
                        pool.wait_ge(stored[u], (b * GROUPS + it + 1) * 16)
                        pool.tensor_tensor(res[:, u, :], z_sb[:, u, :],
                                           x_sb[:, bass.ds(b % 2, 1), bass.ds(it * (UNROLL * QC) + u * QC, QC)]
                                           .rearrange("p a n -> p (a n)"), ALU.add).then_inc(res_ready, 1)

        @block.tensor
        def _(pe):
            pe.wait_ge(consts_loaded, 16 * 15)
            pe.transpose(m_ps[:, 0:P], w_nat[:, 0, :], ident[:, :]).then_inc(w_turned, 1)
            pe.transpose(m_ps[:, P:2 * P], w_nat[:, 1, :], ident[:, :]).then_inc(w_turned, 1)
            pe.transpose(m_ps[0:CI, 2 * P:3 * P], wout_nat[:, :], ident[:, :]).then_inc(w_turned, 1)
            pe.wait_ge(w_ready, 3)
            pe.wait_ge(zeroed, 6)

            def conv_q(b, j, u, g):
                pe.matmul(m_ps[:, :], w_q[:, :],
                          x_sb[:, bass.ds(b % 2, 1), bass.ds(j * QC, QC)].rearrange("p a n -> p (a n)"),
                          start=True, stop=True).then_inc(q_done, 1)

            def max_scores(u, part, g):
                if g is not None:
                    pe.wait_ge(mx_reduced, g * PARTS + (part - 1))
                for half in range(2):
                    key = (part % SUBS) * SUB + half * (SUB // 2)
                    mm = pe.matmul(mx_ps[:, 2 * (part % 2) + half, 0:SUB // 2],
                                   q_hl[:, u, (part // SUBS) * P:(part // SUBS + 1) * P],
                                   k_hi[:, key:key + SUB // 2], start=True, stop=True)
                mm.then_inc(mx_done, 1)

            def max_row(g):
                pe.wait_ge(max_ready, g + 1)
                for q in range(QT):
                    mm = pe.transpose(m_ps[0:1, q * P:(q + 1) * P], neg_max[:, q:q + 1], ident[:, :])
                mm.then_inc(maxrow_done, 1)

            def scores(u, kt):
                pe.matmul(st_ps[:, kt % 2, :], k_hi[:, kt * P:(kt + 1) * P], q_hl[:, u, :],
                          start=True, stop=False)
                pe.matmul(st_ps[:, kt % 2, :], k_lo[:, kt * P:(kt + 1) * P], q_mx[:, u, :],
                          start=False, stop=True).then_inc(st_done, 1)

            def values(kt, g):
                pe.wait_ge(exp_done, g * KT + (kt + 1))
                for q in range(QT):
                    mm = pe.matmul(o_ps[:, q * VW:(q + 1) * VW], probs[:, kt % UNROLL, q * P:(q + 1) * P],
                                   v_t[:, kt, :], start=(kt == 0 and q == 0), stop=(kt == KT - 1),
                                   skip_group_check=True)
                mm.then_inc(pv_done, 1)

            def turn_y(g, more=()):
                wait_apart(pe, (zeroed, 6), [(y_ready, g + 1), *more])
                for q in range(QT):
                    mm = pe.transpose(m_ps[0:CI, q * P:(q + 1) * P], y_sb[:, q, :], ident[:, :])
                mm.then_inc(yt_done, 1)

            def conv_out(g):
                pe.wait_ge(yt_copied, g + 1)
                pe.matmul(m_ps[:, :], w_out[:, :], y_t[:, :], start=True, stop=True).then_inc(z_done, 1)

            def chunk(b, g, i, u, first, last):
                static = isinstance(last, bool)
                i_st = i if not static else None
                for kt in range(KT):
                    if kt == 0:
                        pe.wait_ge(maxrow_low, g + 1)
                    if not (first and kt < 2):
                        pe.wait_ge(exp_done, g * KT + (kt - 1))
                    scores(u, kt)
                    if kt < PARTS and i_st != CHUNKS - 1:
                        if kt == 0:
                            pe.wait_ge(q_low, g + 2)
                        max_scores((u + 1) % UNROLL, kt, g + 1)
                    if kt >= LAG:
                        if kt == LAG and not first:
                            pe.wait_ge(o_copied, g)
                        values(kt - LAG, g)
                    elif not first:
                        values(KT - LAG + kt, g - 1)
                    if kt == 4 and not first:
                        turn_y(g - 1)
                    if kt == 7 and not first:
                        conv_out(g - 1)
                    if kt == 10 and (i_st is None or i_st + 2 < CHUNKS):
                        if not first:
                            pe.wait_ge(z_ready, g + 1)
                        conv_q(b, i + 2, (u + 2) % UNROLL, g + 2)
                    if kt == 14 and i_st != CHUNKS - 1:
                        if i_st is None or i_st + 2 < CHUNKS:
                            pe.wait_ge(q_copied, g + 3)
                            pe.wait_ge(q_low, g + 3)
                        else:
                            pe.wait_ge(z_ready, g + 1)
                        max_row(g + 1)

            def start(b):
                pe.wait_ge(x_loaded, (b + 1) * (16 * XLOADS))
                for n in range(4):
                    with_kv(b, 0, n, first=True)
                with pe.Fori(1, NCONV // 4) as it:
                    for n in range(4):
                        with_kv(b, it, n, first=False)
                g = b * CHUNKS
                pe.wait_ge(z_ready, g + 1)
                conv_q(b, 0, 0, g)
                wait_apart(pe, (zeroed, 6), [(v_biased, b + 1)])
                for kt in range(KT):
                    tr = pe.transpose(mx_ps[:, kt // 8, (kt % 8) * CI:(kt % 8 + 1) * CI],
                                      v_f32[:, kt * P:(kt + 1) * P], ident[0:CI, 0:CI])
                tr.then_inc(v_turned, 1)
                pe.wait_ge(q_copied, g + 1)
                pe.wait_ge(q_low, g + 1)
                conv_q(b, 1, 1, g + 1)
                pe.wait_ge(khi_ready, (b + 1) * 2)
                pe.wait_ge(klo_ready, b + 1)
                pe.wait_ge(v_ready, b + 1)
                for part in range(PARTS):
                    max_scores(0, part, g if part >= 2 else None)
                pe.wait_ge(q_copied, g + 2)
                pe.wait_ge(q_low, g + 2)
                max_row(g)

            def with_kv(b, it, n, first):
                if not first:
                    pe.wait_ge(kv_pooled, b * NCONV + it * 4 + (n - 3))
                pe.matmul(mx_ps[:, n, 0:CONV], w_kv[:, :],
                          x_sb[:, bass.ds(b % 2, 1), bass.ds(it * (4 * CONV) + n * CONV, CONV)]
                          .rearrange("p a n -> p (a n)"), start=True, stop=True).then_inc(kv_done, 1)

            def end(b):
                g = (b + 1) * CHUNKS - 1
                values(KT - 2, g)
                values(KT - 1, g)
                turn_y(g, [(z_ready, g + 1)])
                conv_out(g)

            chunk.start, chunk.end = start, end
            chunk_loop(pe, chunk)

        @block.scalar
        def _(act):
            act.sem_inc(z_ready, 1)
            act.wait_ge(consts_loaded, 16 * 15)
            act.wait_ge(zeroed, 6)
            act.activation(STD, VAR, ACT.Sqrt, bias=EPS).then_inc(std_ready, 1)
            act.wait_ge(w_turned, 3)
            act.copy(w_kv[:, :], m_ps[:, 0:P]).then_inc(w_ready, 1)
            act.copy(w_q[:, :], m_ps[:, P:2 * P]).then_inc(w_ready, 1)
            act.copy(w_out[:, :], m_ps[0:CI, 2 * P:3 * P]).then_inc(w_ready, 1)
            act.wait_ge(consts_ready, 4)

            def take_q(u, g):
                act.wait_ge(q_done, g + 1)
                act.activation(q_hl[:, u, :], m_ps[:, :], ACT.Identity, bias=B_Q)
                act.activation(q_mx[0:CI, u, :], m_ps[0:CI, :], ACT.Identity, bias=B_Q[0:CI]).then_inc(q_copied, 1)

            def take_max(u, g):
                act.wait_ge(maxrow_done, g + 1)
                act.copy(q_mx[ROW_HI:ROW_HI + 1, u, :], m_ps[0:1, :]).then_inc(maxrow_high, 1)

            def take_y(g):
                act.wait_ge(yt_done, g + 1)
                act.copy(y_t[:, :], m_ps[0:CI, :]).then_inc(yt_copied, 1)

            def take_z(u, g):
                act.wait_ge(z_done, g + 1)
                act.wait_ge(res_ready, g + 1)
                act.activation(z_sb[:, u, :], m_ps[:, :], ACT.Identity, bias=OFFSET, scale=INV).then_inc(z_ready, 1)

            def chunk(b, g, i, u, first, last):
                i_st = None if isinstance(last, bool) else i
                before = (u + UNROLL - 1) % UNROLL
                for kt in range(KT):
                    act.wait_ge(st_done, g * KT + (kt + 1))
                    if not (first and kt < UNROLL):
                        act.wait_ge(pv_done, g * KT + (kt - 2))
                    act.activation(probs[:, kt % UNROLL, :], st_ps[:, kt % 2, :], ACT.Exp).then_inc(exp_done, 1)
                    if kt == 4 and not first:
                        take_y(g - 1)
                    if kt == 7 and not first:
                        take_z(before, g - 1)
                    if kt == 10 and (i_st is None or i_st + 2 < CHUNKS):
                        take_q((u + 2) % UNROLL, g + 2)
                    if kt == 14 and i_st != CHUNKS - 1:
                        take_max((u + 1) % UNROLL, g + 1)

            def start(b):
                g = b * CHUNKS
                act.wait_ge(kv_pooled, (b + 1) * NCONV)
                act.activation(k_hi[0:CI, :], kv_raw[0:CI, :], ACT.Identity, bias=B_PHI[0:CI]).then_inc(khi_ready, 1)
                take_q(0, g)
                act.activation(k_hi[CI:P, :], kv_raw[0:CI, :], ACT.Identity, bias=B_PHI[0:CI]).then_inc(khi_ready, 1)
                act.wait_ge(v_turned, b + 1)
                for n in range(3):
                    tiles = min(8, KT - 8 * n)
                    cp = act.copy(v_t[:, 8 * n:8 * n + tiles, 0:CI],
                                  mx_ps[:, n, 0:tiles * CI].rearrange("p (t c) -> p t c", c=CI))
                cp.then_inc(v_ready, 1)
                take_q(1, g + 1)
                take_max(0, g)

            def end(b):
                g = (b + 1) * CHUNKS - 1
                take_y(g)
                take_z(UNROLL - 1, g)

            chunk.start, chunk.end = start, end
            chunk_loop(act, chunk)

        @block.vector
        def _(dve):
            dve.memset(EPS, 1e-5).then_inc(zeroed, 1)
            dve.memset(q_mx[CI:P, :, :].bitcast(F32), 0.0).then_inc(zeroed, 1)
            dve.memset(v_t[:, :, :], 1.0).then_inc(zeroed, 1)
            dve.memset(k_lo[CI:P, :].bitcast(F32), 0.0).then_inc(zeroed, 1)
            dve.wait_ge(zeroed, 4)
            dve.memset(k_lo[ROW_HI:ROW_HI + 1, :].bitcast(F32), 1.0).then_inc(zeroed, 1)
            dve.memset(k_lo[ROW_LO:ROW_LO + 1, :].bitcast(F32), 1.0).then_inc(zeroed, 1)
            dve.wait_ge(std_ready, 1)
            dve.reciprocal(INV, STD).then_inc(consts_ready, 1)
            dve.wait_ge(consts_ready, 1)
            dve.tensor_tensor(INV, INV, GAMMA, ALU.mult).then_inc(consts_ready, 1)
            dve.tensor_tensor(OFFSET, B_W, MEAN, ALU.subtract).then_inc(consts_ready, 1)
            dve.wait_ge(consts_ready, 3)
            dve.scalar_tensor_tensor(OFFSET, OFFSET, INV, BETA, ALU.mult, ALU.add).then_inc(consts_ready, 1)

            def pool_kv(b, it, n):
                dve.wait_ge(kv_done, b * NCONV + it * 4 + (n + 1))
                dve.tensor_reduce(kv_raw[:, bass.ds(it * CONV + n * (CONV // 4), CONV // 4)],
                                  mx_ps[:, n, 0:CONV].rearrange("p (i r j c) -> p i j r c", r=2, c=2, j=WIDTH // 2),
                                  AX.XY, ALU.max).then_inc(kv_pooled, 1)

            def low_q(u, g):
                dve.wait_ge(q_copied, g + 1)
                dve.scalar_tensor_tensor(q_hl[CI:P, u, :], m_ps[CI:P, :], B_Q[CI:P],
                                         q_hl[CI:P, u, :].bitcast(F32), ALU.add, ALU.subtract).then_inc(q_low, 1)

            def reduce_max(part, g):
                dve.wait_ge(mx_done, g * PARTS + (part + 1))
                b0 = 2 * (part % 2)
                dve.tensor_reduce(part_max[:, part:part + 1], mx_ps[:, b0:b0 + 2, 0:SUB // 2],
                                  AX.XY, ALU.max).then_inc(mx_reduced, 1)

            def finish_max(g):
                dve.wait_ge(mx_reduced, (g + 1) * PARTS)
                dve.tensor_reduce(neg_max[:, :], part_max[:, :].rearrange("p (q s) -> p q s", s=SUBS),
                                  AX.X, ALU.max, negate=True).then_inc(max_ready, 1)

            def low_max(u, g):
                dve.wait_ge(maxrow_high, g + 1)
                dve.tensor_tensor(q_mx[ROW_LO:ROW_LO + 1, u, :], m_ps[0:1, :],
                                  q_mx[ROW_HI:ROW_HI + 1, u, :].bitcast(F32), ALU.subtract).then_inc(maxrow_low, 1)

            def divide(g):
                dve.wait_ge(pv_done, (g + 1) * KT)
                dve.tensor_copy(o_sb[:, :], o_ps[:, 0:QT * VW]).then_inc(o_copied, 1)
                dve.wait_ge(o_copied, g + 1)
                o = o_sb[:, :].rearrange("p (q v) -> p q v", v=VW)
                dve.reciprocal(o_rec[:, :], o[:, :, CI]).then_inc(o_inverted, 1)
                dve.wait_ge(o_inverted, g + 1)
                dve.tensor_tensor(y_sb[:, :, :], o[:, :, 0:CI],
                                  o_rec[:, :].rearrange("p (q a) -> p q a", a=1).broadcast_to([P, QT, CI]),
                                  ALU.mult).then_inc(y_ready, 1)

            def chunk(b, g, i, u, first, last):
                i_st = None if isinstance(last, bool) else i
                for kt in range(KT):
                    if kt == 2 and not first:
                        divide(g - 1)
                    if kt < PARTS and i_st != CHUNKS - 1:
                        reduce_max(kt, g + 1)
                    if kt == 11 and (i_st is None or i_st + 2 < CHUNKS):
                        low_q((u + 2) % UNROLL, g + 2)
                    if kt == 12 and i_st != CHUNKS - 1:
                        finish_max(g + 1)
                    if kt == 14 and i_st != CHUNKS - 1:
                        low_max((u + 1) % UNROLL, g + 1)

            def start(b):
                g = b * CHUNKS
                with dve.Fori(0, NCONV // 4) as it:
                    for n in range(4):
                        pool_kv(b, it, n)
                dve.wait_ge(kv_pooled, (b + 1) * NCONV)
                dve.tensor_scalar(v_f32[:, :], kv_raw[CI:P, :], B_G[CI:P], None, ALU.add).then_inc(v_biased, 1)
                dve.wait_ge(khi_ready, b * 2 + 1)
                dve.scalar_tensor_tensor(k_lo[0:CI, :], kv_raw[0:CI, :], B_PHI[0:CI],
                                         k_hi[0:CI, :].bitcast(F32), ALU.add, ALU.subtract).then_inc(klo_ready, 1)
                low_q(0, g)
                low_q(1, g + 1)
                for part in range(PARTS):
                    reduce_max(part, g)
                finish_max(g)
                low_max(0, g)

            def end(b):
                divide((b + 1) * CHUNKS - 1)

            chunk.start, chunk.end = start, end
            chunk_loop(dve, chunk)


def program(nc, a, ident, mask, rgb_mask, out):
    gr = nc.dram_tensor("g_r_padded", (PW, PW, CI), F32).ap()
    ar = nc.dram_tensor("a_padded", (PW, PW), F32).ap()
    x1 = nc.dram_tensor("layer0_out", (FRAMES, CH, HEIGHT, WIDTH), F32).ap()
    p = "L0_conv_"
    nc.disable_value_cache = True
    rgb_fields(nc, a[p + "rgb"].rearrange("o c h w -> (o c) h w"), a[p + "rgb_g_w"], a[p + "rgb_g_b"],
               a[p + "rgb_theta_w"], a[p + "rgb_theta_b"], a[p + "cp_w"], ident, gr, ar)
    layer0(nc, a["x"], gr, ar, x1, ident, mask, rgb_mask,
           *(a[p + n] for n in ("g_w", "g_b", "theta_w", "theta_b", "phi_w", "phi_b", "W_w", "W_b",
                                "rgb_phi_w", "rgb_phi_b", "rgb_W_w", "rgb_W_b", "cp_w")))
    p = "L1_conv_"
    layer1(nc, FRAMES, x1.rearrange("f c h w -> f c (h w)"), out.rearrange("f c h w -> f c (h w)"),
           *(a[p + n] for n in ("g_w", "g_b", "theta_w", "theta_b", "phi_w", "phi_b", "W_w", "W_b",
                                "bn_gamma", "bn_beta", "bn_mean", "bn_var")), ident)


def neighbour_mask(order, frames, inside, outside):
    taps = {-3: (-3, 0, 3), -1: (-1, 0, 1), 0: (-3, -1, 0, 1, 3), 1: (-1, 0, 1), 3: (-3, 0, 3)}
    one = np.full((TILE_COLS, len(order), frames, TILE_COLS + 6), outside, np.float32)
    for q in range(TILE_COLS):
        for j, dy in enumerate(order):
            for dx in taps[dy]:
                one[q, j, :, q + 3 + dx] = inside
    return np.tile(one.reshape(TILE_COLS, -1), (FRAMES, 1))


_L0 = ["rgb", "g_w", "g_b", "theta_w", "theta_b", "phi_w", "phi_b", "W_w", "W_b", "rgb_g_w", "rgb_g_b",
       "rgb_theta_w", "rgb_theta_b", "rgb_phi_w", "rgb_phi_b", "rgb_W_w", "rgb_W_b", "cp_w"]
_L1 = ["g_w", "g_b", "theta_w", "theta_b", "phi_w", "phi_b", "W_w", "W_b",
       "bn_gamma", "bn_beta", "bn_mean", "bn_var"]
_INS = ["x"] + ["L0_conv_" + n for n in _L0] + ["L1_conv_" + n for n in _L1]


def kernel(**inputs):
    import concourse.bacc as _bacc
    from concourse.bass_utils import run_bass_kernel_spmd as _run

    nc = _bacc.Bacc("TRN2", target_bir_lowering=False, num_devices=1)
    arrays, aps = {}, {}

    def given(name, array):
        arrays[f"in_{name}_dram"] = array
        return nc.dram_tensor(f"in_{name}_dram", array.shape, mybir.dt.from_np(array.dtype),
                              kind="ExternalInput").ap()

    for name in _INS:
        aps[name] = given(name, np.ascontiguousarray(inputs[name]))
    ident = given("identity", np.eye(P, dtype=np.float32))
    mask = given("mask", neighbour_mask((-3, -1, 0, 1, 3), FRAMES, 0.0, -1.0e30))
    rgb_mask = given("rgb_mask", neighbour_mask((-3, 0, 3, -1, 1), 1, 1.0, 0.0))
    out = nc.dram_tensor("out_0_dram", (FRAMES, CH, HEIGHT, WIDTH), F32, kind="ExternalOutput").ap()
    program(nc, aps, ident, mask, rgb_mask, out)
    r = _run(nc, [arrays], core_ids=[0])
    return r.results[0]["out_0_dram"]
```

```python
import math
from contextlib import ExitStack

import numpy as np

import concourse.bass as bass
from concourse import mybir

F32 = mybir.dt.float32
F16, BF16 = mybir.dt.float16, mybir.dt.bfloat16
F32R = mybir.dt.float32r
ALU = mybir.AluOpType
ACT = mybir.ActivationFunctionType
AX = mybir.AxisListType

P = 128
CH, CI = 128, 64
HEIGHT = WIDTH = 96
POS = HEIGHT * WIDTH
FRAMES = 8
PW = WIDTH + 6
TILE_COLS = 16
ROWS = (-3, 3, -1, 0, 1)
TAPROWS = len(ROWS)
GR = CI + 1
TAPS = 17
RING = 8
QC = 512
UNROLL = 3


def column(vector):
    return vector.rearrange("(c one) -> c one", one=1)


def windows(row, width, count):
    k = row.shape[1]
    return bass.AP(row.tensor, row.offset, [[k, width], [TILE_COLS * k, count], [1, k]])


def row_windows(rows, width, count):
    part, frames, step = rows.ap
    return bass.AP(rows.tensor, rows.offset, [part, [TILE_COLS, count], frames, [1, width]])


def wait_apart(eng, passed, waits):
    waits = [(s, v if isinstance(v, int) else eng.snap(eng.to_reg(v))) for s, v in waits]
    eng.wait_ge(*passed)
    for s, v in waits:
        eng.wait_ge(s, v)


def rgb_fields(nc, rgb, g_w, g_b, theta_w, theta_b, cp_w, identity_dram, gr_dram):
    ROWS = 6
    STEPS = HEIGHT // ROWS
    with ExitStack() as ctx:
        def sb(name, shape, dt=F32):
            return ctx.enter_context(nc.sbuf_tensor(name, shape, dt))

        def sem(name):
            return ctx.enter_context(nc.semaphore(name))

        x_sb = sb("rgb_sb", [P, 2, ROWS, WIDTH])
        zeros = sb("rgb_zeros", [PW, 3 * GR])
        ident = sb("rgb_ident", [P, P])
        g_nat = sb("rg_nat", [CI, CH])
        th_nat = sb("rth_nat", [CI, CH])
        vec = sb("rgb_vec", [CI, 2])
        bias = sb("rg_bias", [WIDTH, GR])
        w_g = sb("rw_g", [CH, GR])
        g_sb = sb("rg_sb", [WIDTH, 2, ROWS, GR])
        g_ps = ctx.enter_context(nc.psum_tensor("rg_ps", [P, 2, 512], F32))
        w_ps = ctx.enter_context(nc.psum_tensor("rw_ps", [P, 512], F32))

        consts = sem("r_consts")
        zeroed = sem("r_zeroed")
        padded = sem("r_padded")
        loaded = [sem(f"r_loaded{u}") for u in range(2)]
        prepared = sem("r_prepared")
        w_ready = sem("r_w_ready")
        g_done = sem("r_g_done")
        g_ready = sem("r_g_ready")
        g_stored = [sem(f"r_g_stored{u}") for u in range(2)]

        block = ctx.enter_context(nc.Block())

        @block.sync
        def _(sp):
            sp.dma_start(ident[:, :], identity_dram).then_inc(consts, 16)
            sp.dma_start(g_nat[:, :], g_w).then_inc(consts, 16)
            sp.dma_start(th_nat[:, :], theta_w).then_inc(consts, 16)
            sp.dma_start(vec[:, 0:1], column(cp_w[0:CI])).then_inc(consts, 16)
            sp.dma_start(vec[:, 1:2], column(theta_b)).then_inc(consts, 16)
            sp.dma_start(bias[:, 0:CI], g_b.rearrange("(o c) -> o c", o=1).broadcast_to([WIDTH, CI])
                         ).then_inc(consts, 16)

            def load(step, u):
                sp.dma_start(x_sb[:, u, :, :], rgb[:, bass.ds(step * ROWS, ROWS), :]).then_inc(loaded[u], 16)

            def store(step, u):
                sp.wait_ge(g_ready, step + 2)
                sp.dma_start(gr_dram[bass.ds(step * ROWS + 3, ROWS), 3:3 + WIDTH, :].rearrange("r c k -> c r k"),
                             g_sb[:, u, :, :]).then_inc(g_stored[u], 16)

            load(0, 0)
            load(1, 1)
            sp.wait_ge(zeroed, 1)
            for r0 in (0, 3 + HEIGHT):
                sp.dma_start(gr_dram[r0:r0 + 3, :, :].rearrange("r c k -> c r k"),
                             zeros[:, :].rearrange("c (r k) -> c r k", k=GR)).then_inc(padded, 16)
            for c0 in (0, 3 + WIDTH):
                sp.dma_start(gr_dram[3:3 + HEIGHT, c0:c0 + 3, :], zeros[0:HEIGHT, :].rearrange("r (c k) -> r c k", k=GR)
                             ).then_inc(padded, 16)
            with sp.Fori(0, STEPS // 2 - 1) as it:
                for u in range(2):
                    store(2 * it + u, u)
                    load(2 * it + 2 + u, u)
            for u in range(2):
                store(STEPS - 2 + u, u)
            sp.wait_ge(padded, 16 * 4)
            for u in range(2):
                sp.wait_ge(g_stored[u], 16 * (STEPS // 2 + 1))

        @block.tensor
        def _(pe):
            pe.wait_ge(consts, 16 * 6)
            pe.transpose(w_ps[:, 0:CI], g_nat[:, :], ident[0:CI, 0:CI])
            pe.matmul(w_ps[:, CI:GR], th_nat[:, :], vec[:, 0:1], start=True, stop=True)
            pe.matmul(w_ps[0:WIDTH, GR:GR + 1], vec[:, 1:2].broadcast_to([CI, WIDTH]), vec[:, 0:1],
                      start=True, stop=True).then_inc(prepared, 1)
            pe.wait_ge(w_ready, 1)
            with pe.Fori(0, STEPS // 2) as it:
                for u in range(2):
                    pe.wait_ge(loaded[u], (it + 1) * 16)
                    pe.wait_ge(g_ready, it * 2 + (u + 1))
                    for r in range(ROWS):
                        mm = pe.matmul(g_ps[0:WIDTH, u, r * GR:(r + 1) * GR], x_sb[:, u, r, :], w_g[:, :],
                                       start=True, stop=True)
                    mm.then_inc(g_done, 1)

        @block.scalar
        def _(act):
            act.wait_ge(prepared, 1)
            act.copy(bias[:, CI:GR], w_ps[0:WIDTH, GR:GR + 1])
            act.copy(w_g[:, :], w_ps[:, 0:GR]).then_inc(w_ready, 1)

        @block.vector
        def _(dve):
            dve.memset(zeros[:, :], 0.0).then_inc(zeroed, 1)
            dve.sem_inc(g_ready, 1)
            for u in range(2):
                dve.sem_inc(g_stored[u], 16)
            dve.wait_ge(consts, 16 * 6)
            dve.wait_ge(w_ready, 1)
            with dve.Fori(0, STEPS // 2) as it:
                for u in range(2):
                    dve.wait_ge(g_done, it * 2 + (u + 1))
                    dve.wait_ge(g_stored[u], (it + 1) * 16)
                    dve.tensor_tensor(g_sb[:, u, :, :], g_ps[0:WIDTH, u, 0:ROWS * GR].rearrange("p (r k) -> p r k", k=GR),
                                      bias[:, :].rearrange("p (o k) -> p o k", o=1).broadcast_to([WIDTH, ROWS, GR]),
                                      ALU.add).then_inc(g_ready, 1)


def layer0(nc, x_dram, gr_dram, x1_dram, identity_dram, mask_dram, rgb_mask_dram,
           g_w, g_b, theta_w, theta_b, phi_w, phi_b, W_w, W_b,
           rgb_phi_w, rgb_phi_b, rgb_W_w, rgb_W_b, cp_w):
    F = FRAMES
    WIN = TILE_COLS + 6
    TILES = WIDTH // TILE_COLS
    ROWKEYS = F * WIN
    NKEYS = TAPROWS * ROWKEYS
    HF = F // 2
    KB = HF * WIN
    BLOCKS = 2 * TAPROWS
    RK = TAPROWS * WIN
    LEAD = 4
    HALF = HF * WIDTH
    BIG = 3.0e38
    UR = RING
    XR = 4
    RP = 3
    RF = 4
    GP = 3
    LIFT = 12 * math.log(2.0)

    with ExitStack() as ctx:
        def sb(name, shape, dt=F32):
            return ctx.enter_context(nc.sbuf_tensor(name, shape, dt))

        def sem(name):
            return ctx.enter_context(nc.semaphore(name))

        ident = sb("ident0", [P, P])
        mask = sb("mask", [P, NKEYS])
        rgb_mask = sb("rgb_mask", [RK, P])
        nat = sb("nat", [P, 5, CH])
        vec = sb("vec", [CI, 2])
        cols = sb("cols0", [P, 5])
        B_TH, B_PH, B_OUT, B_OUT_R, B_B = (cols[:, n:n + 1] for n in range(5))
        w_th = sb("w_th", [P, P])
        w_ph = sb("w_ph", [P, 2, CI])
        w_g = sb("w_g0", [CH, CI])
        w_out = sb("w_out0", [P, CH])
        zeros = sb("zeros0", [P, 2 * CI])
        g_bias = sb("g_bias", [KB, TILES, 2, CI])

        th_hi = sb("th_hi", [P, RING, F, PW], F32R)
        th_lo = sb("th_lo", [CI, RING, F, PW], F32R)
        g_t = sb("g_t", [KB, RING, TILES, 2, GP, CI], BF16)
        g_sum = sb("g_sum", [KB, 2, 6 * CI])
        g_rest = sb("g_rest", [KB, 2, 6 * CI])
        x_pad = sb("x_pad", [P, 2, F, PW])
        x_win = sb("x_win", [P, TILES, 2, KB])
        x_row = sb("x_row", [P, XR, F, WIDTH])
        ph_hl = sb("ph_hl", [P, 2, TILES, F, TILE_COLS], F32R)
        b_all = sb("b_all", [RK, 2, TILES, F, TILE_COLS])
        gr_win = sb("gr_win", [RK, 2, TILES, GR])
        neg_s = sb("neg_s", [P, 2, NKEYS])
        neg_max = sb("neg_max0", [P, 2])
        lifted = sb("lifted", [P, 2])
        probs = sb("probs0", [P, RP, NKEYS])
        probs_low = sb("probs_low0", [P, RP, NKEYS], F16)
        sums = sb("sums", [P, TILES])
        factor = sb("factor", [P, TILES, GP + 1])
        f_relu = sb("f_relu", [RK, 2, P])
        f_rgb = sb("f_rgb", [RK, RF, P])
        p_t = sb("p_t", [KB, 2, BLOCKS, P], BF16)
        p_t_low = sb("p_t_low", [KB, 2, BLOCKS, P], F16)
        ident16 = sb("ident16", [P, P], BF16)
        ident16f = sb("ident16f", [P, P], F16)
        y_sb = sb("y_sb0", [P, TILES, GP + 2, CI])
        y_t = sb("y_t0", [P, 3 * P])
        z_row = sb("z_row", [P, 2, F, WIDTH])
        o_row = sb("o_row", [P, 2, F, WIDTH])

        s_ps = ctx.enter_context(nc.psum_tensor("s_ps", [P, 2, 512], F32))
        t_ps = ctx.enter_context(nc.psum_tensor("t_ps", [P, 3, 1024], BF16))
        y_ps = ctx.enter_context(nc.psum_tensor("y_ps", [P, 512], F32))
        ma_ps = ctx.enter_context(nc.psum_tensor("ma_ps", [P, 512], F32))
        mb_ps = ctx.enter_context(nc.psum_tensor("mb_ps", [P, 512], F32))

        consts = sem("consts0")
        biased = sem("biased0")
        patched = sem("patched0")
        zeroed = sem("zeroed0")
        th_zeroed = sem("th_zeroed")
        vecs_done = sem("vecs_done")
        w_turned = sem("w_turned0")
        w_ready = sem("w_ready0")
        pad_loaded = [sem(f"pad_loaded{u}") for u in range(2)]
        row_loaded = [sem(f"row_loaded{u}") for u in range(XR)]
        win_loaded = [sem(f"win_loaded{u}") for u in range(2)]
        win_copied = sem("win_copied")
        th_done = sem("th_done")
        th_high = sem("th_high")
        th_ready = sem("th_ready")
        g_done = sem("g_done")
        g_summed = sem("g_summed")
        g_rested = sem("g_rested")
        g_high = sem("g_high")
        g_ready = sem("g_ready")
        ph_done = sem("ph_done")
        ph_high = sem("ph_high")
        ph_ready = sem("ph_ready")
        ident_cast = sem("ident_cast")
        b_ready = sem("b_ready")
        s_done = sem("s_done")
        s_masked = sem("s_masked")
        max_lifted = sem("max_lifted")
        low_ready = sem("low_ready")
        exp_done = sem("exp_done0")
        relu_done = sem("relu_done")
        f_ready = sem("f_ready")
        t_done = sem("t_done")
        t_act = sem("t_act")
        t_dve = sem("t_dve")
        pv_done = sem("pv_done0")
        inverted = sem("inverted0")
        y_divided = sem("y_divided")
        y_ready = sem("y_ready0")
        yt_done = sem("yt_done0")
        yt_copied = sem("yt_copied0")
        z_done = sem("z_done0")
        z_ready = sem("z_ready0")
        o_ready = sem("o_ready")
        stored = [sem(f"stored0{u}") for u in range(2)]
        WIN_DMAS = TAPROWS

        def f_slot(ct, u):
            return (u * TILES + ct) % RF
        NCONST = 19

        def loads_seen(r, u, ahead, ring, dmas=1):
            return (r - u) * (16 * dmas // ring) + 16 * dmas * ((u + ahead) // ring + 1)

        def high(tensor):
            return tensor.bitcast(BF16).rearrange("p (n half) -> p n half", half=2)[:, :, 1]

        def rows_loop(eng, step):
            for u in range(UR):
                step(u, u, u)
            with eng.Fori(1, HEIGHT // UR - 1) as it:
                for u in range(UR):
                    step(it * UR + u, u, None)
            for u in range(UR):
                r = HEIGHT - UR + u
                step(r, u, r)

        block = ctx.enter_context(nc.Block())

        @block.sync
        def _(sp):
            def load_pad(t, par):
                sp.dma_start(x_pad[:, par, :, 3:3 + WIDTH],
                             x_dram[:, :, bass.ds(t, 1), :].rearrange("f c r w -> c f (r w)")).then_inc(pad_loaded[par], 16)

            def load_row(r, slot):
                sp.dma_start(x_row[:, slot, :, :],
                             x_dram[:, :, bass.ds(r, 1), :].rearrange("f c r w -> c f (r w)")).then_inc(row_loaded[slot], 16)

            def load_window(r, par):
                for j, dy in enumerate(sorted(ROWS)):
                    src = gr_dram[bass.ds(r + 3 + dy, 1), :, :].rearrange("r c k -> (r c) k")
                    sp.dma_start(gr_win[j * WIN:(j + 1) * WIN, par, :, :], windows(src, WIN, TILES)
                                 ).then_inc(win_loaded[par], 16)

            sp.dma_start(ident[:, :], identity_dram).then_inc(consts, 16)
            for n, w in enumerate((theta_w, theta_w, phi_w, phi_w)):
                half = n % 2
                sp.dma_start(nat[half * CI:(half + 1) * CI, n // 2, :], w).then_inc(consts, 16)
            sp.dma_start(nat[0:CI, 2, :], g_w).then_inc(consts, 16)
            sp.dma_start(nat[0:CI, 4, :], rgb_phi_w).then_inc(consts, 16)
            sp.dma_start(nat[:, 3, CI:CH], W_w).then_inc(consts, 16)
            sp.dma_start(nat[:, 3, 0:CI], rgb_W_w).then_inc(consts, 16)
            sp.dma_start(vec[:, 0:1], column(cp_w[CI:2 * CI])).then_inc(consts, 16)
            sp.dma_start(vec[:, 1:2], column(rgb_phi_b)).then_inc(consts, 16)
            for half in range(2):
                sp.dma_start(B_TH[half * CI:(half + 1) * CI], column(theta_b)).then_inc(consts, 16)
                sp.dma_start(B_PH[half * CI:(half + 1) * CI], column(phi_b)).then_inc(consts, 16)
            sp.dma_start(B_OUT, column(W_b)).then_inc(consts, 16)
            sp.dma_start(B_OUT_R, column(rgb_W_b)).then_inc(consts, 16)
            sp.dma_start(mask[:, :], mask_dram).then_inc(consts, 16)
            sp.dma_start(rgb_mask[:, :], rgb_mask_dram).then_inc(consts, 16)
            sp.dma_start(g_bias[:, :, :, :].rearrange("p t h k -> p (t h) k"),
                         g_b.rearrange("(o a c) -> o a c", o=1, a=1).broadcast_to([KB, 2 * TILES, CI])
                         ).then_inc(biased, 16)
            load_row(0, 0)
            load_row(1, 1)
            sp.wait_ge(biased, 16)
            sp.wait_ge(zeroed, 1)
            for f in range(HF):
                sp.dma_start(g_bias[f * WIN:f * WIN + 3, 0, :, :],
                             zeros[0:3, :].rearrange("p (h k) -> p h k", k=CI)).then_inc(patched, 16)
                sp.dma_start(g_bias[f * WIN + WIN - 3:(f + 1) * WIN, TILES - 1, :, :],
                             zeros[0:3, :].rearrange("p (h k) -> p h k", k=CI)).then_inc(patched, 16)
            sp.wait_ge(zeroed, 2)
            load_pad(0, 0)
            load_pad(1, 1)
            load_window(0, 0)
            for t in range(2, LEAD):
                sp.wait_ge(th_done, 2 * (t - 1))
                sp.wait_ge(win_copied, 2 * (t - 1))
                load_pad(t, t % 2)

            def step(r, u, r_st):
                if r_st is None or r_st + LEAD < HEIGHT:
                    sp.wait_ge(th_done, (r + (LEAD - 1)) * 2)
                    sp.wait_ge(win_copied, (r + (LEAD - 1)) * 2)
                    load_pad(r + LEAD, u % 2)
                if r_st is None or r_st >= 2:
                    sp.wait_ge(o_ready, r - 1 + 2)
                    sp.dma_start(x1_dram[:, :, bass.ds(r - 2, 1), :].rearrange("f c r w -> c f (r w)"),
                                 o_row[:, u % 2, :, :]).then_inc(stored[u % 2], 16)
                if r_st is None or r_st + 2 < HEIGHT:
                    load_row(r + 2, (u + 2) % XR)
                if r_st is None or r_st + 1 < HEIGHT:
                    if r_st != 0:
                        sp.wait_ge(pv_done, r * TILES)
                    load_window(r + 1, (u + 1) % 2)

            rows_loop(sp, step)
            for r in (HEIGHT, HEIGHT + 1):
                sp.wait_ge(o_ready, r - 1 + 2)
                sp.dma_start(x1_dram[:, :, r - 2:r - 1, :].rearrange("f c r w -> c f (r w)"),
                             o_row[:, r % 2, :, :]).then_inc(stored[r % 2], 16)
            for u in range(2):
                sp.wait_ge(stored[u], 16 * (HEIGHT // 2 + 1))

        @block.tensor
        def _(pe):
            pe.wait_ge(consts, 16 * NCONST)
            pe.transpose(ma_ps[:, 0:P], nat[:, 0, :], ident[:, :]).then_inc(w_turned, 1)
            pe.transpose(ma_ps[:, P:2 * P], nat[:, 1, :], ident[:, :]).then_inc(w_turned, 1)
            pe.transpose(ma_ps[:, 2 * P:2 * P + CI], nat[0:CI, 2, :], ident[0:CI, 0:CI]).then_inc(w_turned, 1)
            pe.transpose(ma_ps[:, 3 * P:4 * P], nat[:, 3, :], ident[:, :]).then_inc(w_turned, 1)
            pe.matmul(mb_ps[:, 0:CI], nat[0:CI, 4, :], vec[:, 0:1].broadcast_to([CI, CI]), start=True, stop=True)
            pe.matmul(mb_ps[:, CI:CI + 1], vec[:, 1:2].broadcast_to([CI, P]), vec[:, 0:1], start=True, stop=True
                      ).then_inc(vecs_done, 1)
            pe.wait_ge(w_ready, 8)
            pe.wait_ge(ident_cast, 2)

            def conv_th(h, par):
                pe.matmul(mb_ps[:, 0:HALF], w_th[:, :], x_pad[:, par, h * HF:(h + 1) * HF, 3:3 + WIDTH],
                          start=True, stop=True).then_inc(th_done, 1)

            def conv_g(h):
                for n in range(6):
                    ct, hf = 3 * h + n // 2, n % 2
                    mm = pe.matmul(mb_ps[0:KB, n * CI:(n + 1) * CI],
                                   x_win[:, ct, hf, :],
                                   w_g[:, :], start=True, stop=True)
                mm.then_inc(g_done, 1)

            def conv_ph(h, slot, bank):
                pe.matmul(bank[:, 0:HALF], w_ph[:, :, :].rearrange("p a k -> p (a k)"), x_row[:, slot, h * HF:(h + 1) * HF, :],
                          start=True, stop=True).then_inc(ph_done, 1)

            for t in range(LEAD):
                pe.wait_ge(pad_loaded[t % 2], 16 * (t // 2 + 1))
                for h in range(2):
                    if t + h > 0:
                        pe.wait_ge(g_summed if h == 0 else th_ready, 2 * t + h)
                    conv_th(h, t % 2)
                pe.wait_ge(win_copied, 2 * (t + 1))
                for h in range(2):
                    pe.wait_ge(th_ready if h == 0 else g_summed, 2 * t + (2 if h == 0 else 1))
                    conv_g(h)
            pe.wait_ge(row_loaded[0], 16)
            conv_ph(0, 0, ma_ps)
            pe.wait_ge(g_summed, 2 * LEAD)
            conv_ph(1, 0, mb_ps)
            pe.wait_ge(ph_ready, 2)

            def rows_of(u):
                return ROWS if (u - 3) % RING < (u + 3) % RING else (3, -3) + ROWS[2:]

            def scores(ct, u):
                q = ph_hl[:, u % 2, ct, :, :].rearrange("p f c -> p (f c)")
                q_hi = ph_hl[0:CI, u % 2, ct, :, :].rearrange("p f c -> p (f c)")
                c0 = ct * TILE_COLS
                outer, mid = [(u + d) % RING for d in rows_of(u)[0:2]], (u - 1) % RING * F

                def frames(th, at, n):
                    return th[:, :, :, c0:c0 + WIN].rearrange("p a f c -> p (a f) c")[:, at:at + n, :]

                def both_outer(th):
                    return th[:, outer[0]:outer[1] + 1:outer[1] - outer[0], :, c0:c0 + WIN]

                pieces = [(0, 0, 2 * F, both_outer), (0, 2 * F, HF, lambda th: frames(th, mid, HF))]
                left, at, done = HF + 2 * F, mid + HF, 0
                while left:
                    n = min(left, RING * F - at)
                    pieces.append((1, done, n, lambda th, at=at, n=n: frames(th, at, n)))
                    left, at, done = left - n, (at + n) % (RING * F), done + n
                for bank, at, n, of in pieces:
                    o = s_ps[:, bank, at * WIN:(at + n) * WIN]
                    pe.matmul(o, q, of(th_hi), start=True, stop=False)
                    mm = pe.matmul(o, q_hi, of(th_lo), start=False, stop=True)
                mm.then_inc(s_done, 1)

            def turned(low, k):
                bank, at = (int(low), k) if k < 8 else (2, 2 * low + k - 8)
                o = t_ps[0:KB, bank, at * P:(at + 1) * P]
                return o.bitcast(F16) if low else o

            def turn_probs(par):
                for k in range(8):
                    mm = pe.transpose(turned(False, k), high(probs[:, par, :])[:, k * KB:(k + 1) * KB], ident16[:, :])
                mm.then_inc(t_done, 1)
                for k in range(8):
                    mm = pe.transpose(turned(True, k), probs_low[:, par, k * KB:(k + 1) * KB], ident16f[:, :])
                mm.then_inc(t_done, 1)
                for k in range(8, BLOCKS):
                    pe.transpose(turned(False, k), high(probs[:, par, :])[:, k * KB:(k + 1) * KB], ident16[:, :])
                    mm = pe.transpose(turned(True, k), probs_low[:, par, k * KB:(k + 1) * KB], ident16f[:, :])
                mm.then_inc(t_done, 1)

            def values(ct, u):
                for k in range(BLOCKS):
                    slot = (u + rows_of(u)[k // 2]) % RING
                    for p, parts in ((p_t, GP), (p_t_low, GP - 1)):
                        pe.matmul(y_ps[:, 0:parts * CI], p[:, ct % 2, k, :],
                                  g_t[:, slot, ct, k % 2, 0:parts, :].rearrange("p n k -> p (n k)"),
                                  start=(k == 0 and p is p_t), stop=(k == BLOCKS - 1),
                                  skip_group_check=True)
                pe.matmul(y_ps[:, GP * CI:(GP + 1) * CI], f_rgb[:, f_slot(ct, u), :], gr_win[:, u % 2, ct, 0:CI],
                          start=False, stop=True, skip_group_check=True).then_inc(pv_done, 1)

            def turn_y(h):
                for n in range(3):
                    mm = pe.transpose(ma_ps[:, n * P:(n + 1) * P],
                                      y_sb[:, 3 * h + n, GP:GP + 2, :].rearrange("p a k -> p (a k)"), ident[:, :])
                mm.then_inc(yt_done, 1)

            def conv_out():
                pe.matmul(ma_ps[:, 0:3 * P], w_out[:, :], y_t[:, :], start=True, stop=True).then_inc(z_done, 1)

            def job_a(r, ct, u, r_st):
                back = r_st != 0
                ahead = r_st != HEIGHT - 1
                if ct == 0 and back:
                    if r_st == 1:
                        pe.wait_ge(ph_ready, 3)
                    else:
                        pe.wait_ge(z_ready, r * 2 - 2)
                    pe.wait_ge(y_ready, r * TILES - 3)
                    turn_y(0)
                if ct == 1 and back:
                    pe.wait_ge(yt_copied, r * 2 - 1)
                    conv_out()
                if ct == 2 and ahead:
                    if back:
                        pe.wait_ge(z_ready, r * 2 - 1)
                    else:
                        pe.wait_ge(ph_ready, 1)
                    pe.wait_ge(row_loaded[(u + 1) % XR], loads_seen(r, u, 1, XR))
                    conv_ph(0, (u + 1) % XR, ma_ps)
                if ct == 4 and back:
                    if ahead:
                        pe.wait_ge(ph_ready, r * 2 + 3)
                    else:
                        pe.wait_ge(z_ready, r * 2 - 1)
                    pe.wait_ge(y_ready, r * TILES)
                    turn_y(1)
                if ct == 5 and back:
                    pe.wait_ge(yt_copied, r * 2)
                    conv_out()

            def job_b(r, ct, u, r_st):
                more = r_st is None or r_st + LEAD < HEIGHT
                ahead = r_st != HEIGHT - 1
                if more and ct == 0:
                    pe.wait_ge(ph_ready, r * 2 + 2)
                    pe.wait_ge(pad_loaded[u % 2], loads_seen(r, u, LEAD, 2))
                    conv_th(0, u % 2)
                if more and ct == 1:
                    pe.wait_ge(th_ready, (r + LEAD) * 2 + 1)
                    conv_th(1, u % 2)
                if more and ct == 2:
                    pe.wait_ge(th_ready, (r + LEAD) * 2 + 2)
                    pe.wait_ge(win_copied, (r + (LEAD + 1)) * 2)
                    conv_g(0)
                if more and ct == 3:
                    pe.wait_ge(g_summed, (r + LEAD) * 2 + 1)
                    conv_g(1)
                if ahead and ct == 4:
                    if more:
                        pe.wait_ge(g_summed, (r + LEAD) * 2 + 2)
                    else:
                        pe.wait_ge(ph_ready, r * 2 + 2)
                    conv_ph(1, (u + 1) % XR, mb_ps)

            def turn_tile(n, ct):
                pe.wait_ge(low_ready, n + 1)
                if not (isinstance(n, int) and n == 0):
                    pe.wait_ge(t_act, n)
                    pe.wait_ge(t_dve, n)
                turn_probs(ct % RP)

            def value_tile(n, ct, r, u):
                pe.wait_ge(f_ready, n + 1)
                pe.wait_ge(t_act, n + 1)
                pe.wait_ge(t_dve, n + 1)
                if not (isinstance(n, int) and n == 0):
                    pe.wait_ge(y_divided, n)
                if ct == 0:
                    pe.wait_ge(g_ready, (r + LEAD) * 2)
                    pe.wait_ge(g_high, min(r + LEAD, HEIGHT) * 4 if isinstance(r, int) else (r + LEAD) * 4)
                    pe.wait_ge(win_loaded[u % 2], loads_seen(r, u, 0, 2, WIN_DMAS))
                values(ct, u)

            def step(r, u, r_st):
                for ct in range(TILES):
                    n = r * TILES + ct
                    n_st = None if r_st is None else r_st * TILES + ct
                    if ct == 0:
                        pe.wait_ge(th_ready, (r + LEAD) * 2)
                        pe.wait_ge(ph_ready, r * 2 + 2)
                    if n_st != 0:
                        pe.wait_ge(s_masked, n)
                    scores(ct, u)
                    if n_st is None or n_st >= 2:
                        turn_tile(n - 2, (ct - 2) % TILES)
                    job_a(r, ct, u, r_st)
                    job_b(r, ct, u, r_st)
                    if n_st is None or n_st >= 3:
                        if ct >= 3:
                            value_tile(n - 3, ct - 3, r, u)
                        else:
                            value_tile(n - 3, ct + TILES - 3, r - 1, (u - 1) % UR)

            rows_loop(pe, step)
            n = HEIGHT * TILES
            turn_tile(n - 2, TILES - 2)
            value_tile(n - 3, TILES - 3, HEIGHT - 1, UR - 1)
            turn_tile(n - 1, TILES - 1)
            value_tile(n - 2, TILES - 2, HEIGHT - 1, UR - 1)
            value_tile(n - 1, TILES - 1, HEIGHT - 1, UR - 1)
            pe.wait_ge(z_ready, 2 * HEIGHT - 2)
            turn_y(0)
            pe.wait_ge(yt_copied, 2 * HEIGHT - 1)
            conv_out()
            pe.wait_ge(z_ready, 2 * HEIGHT - 1)
            pe.wait_ge(y_ready, n)
            turn_y(1)
            pe.wait_ge(yt_copied, 2 * HEIGHT)
            conv_out()

        @block.scalar
        def _(act):
            act.wait_ge(consts, 16 * NCONST)
            act.copy(ident16[:, :], ident[:, :]).then_inc(ident_cast, 1)
            act.copy(ident16f[:, :], ident[:, :]).then_inc(ident_cast, 1)
            act.wait_ge(w_turned, 4)
            act.copy(w_th[:, :], ma_ps[:, 0:P]).then_inc(w_ready, 1)
            act.copy(w_ph[:, 0, :], ma_ps[:, P:P + CI]).then_inc(w_ready, 1)
            act.copy(w_g[:, :], ma_ps[:, 2 * P:2 * P + CI]).then_inc(w_ready, 1)
            act.copy(w_out[CI:P, :], ma_ps[CI:P, 3 * P:4 * P]).then_inc(w_ready, 1)
            act.mul(w_out[0:CI, :], ma_ps[0:CI, 3 * P:4 * P], 1.0 / TAPS).then_inc(w_ready, 1)
            act.wait_ge(vecs_done, 1)
            act.copy(w_ph[:, 1, :], mb_ps[:, 0:CI]).then_inc(w_ready, 1)
            act.copy(B_B, mb_ps[:, CI:CI + 1]).then_inc(w_ready, 1)
            act.wait_ge(w_ready, 8)
            act.wait_ge(th_zeroed, 1)

            def take_th(h, slot, count):
                act.wait_ge(th_done, count)
                act.activation(th_hi[:, bass.ds(slot, 1), h * HF:(h + 1) * HF, 3:3 + WIDTH]
                               .rearrange("p a f c -> p (a f) c"),
                               mb_ps[:, 0:HALF].rearrange("p (f c) -> p f c", c=WIDTH),
                               ACT.Identity, bias=B_TH).then_inc(th_high, 1)

            def take_ph(h, par, bank, count, row):
                act.wait_ge(ph_done, count)
                if not (isinstance(row, int) and row < 2):
                    act.wait_ge(f_ready, (row - 1) * TILES)
                for low, end in ((0, CI), (CI, RK)):
                    b = act.activation(b_all[low:end, par, :, h * HF:(h + 1) * HF, :].rearrange("p t f c -> p f t c"),
                                       bank[CI:CI + end - low, 0:HALF].rearrange("p (f t c) -> p f t c", f=HF, c=TILE_COLS),
                                       ACT.Identity, bias=B_B[low:end])
                b.then_inc(b_ready, 1)
                act.activation(ph_hl[0:CI, par, :, h * HF:(h + 1) * HF, :].rearrange("p t f c -> p f t c"),
                               bank[0:CI, 0:HALF].rearrange("p (f t c) -> p f t c", f=HF, c=TILE_COLS),
                               ACT.Identity, bias=B_PH[0:CI]).then_inc(ph_high, 1)

            def g_part(h, slot, n):
                return g_t[:, slot, 3 * h:3 * h + 3, :, n, :].rearrange("p t h k -> p (t h) k")

            def take_g_high(h, slot, count):
                act.wait_ge(g_summed, count)
                act.copy(g_part(h, slot, 0), high(g_sum[:, h, :]).rearrange("p (a k) -> p a k", k=CI)).then_inc(g_high, 1)
                act.wait_ge(g_rested, count)
                act.copy(g_part(h, slot, 1), high(g_rest[:, h, :]).rearrange("p (a k) -> p a k", k=CI)).then_inc(g_high, 1)

            for t in range(LEAD):
                for h in range(2):
                    take_th(h, t, 2 * t + h + 1)
                for h in range(2):
                    take_g_high(h, t, 2 * t + h + 1)
            for h, bank in enumerate((ma_ps, mb_ps)):
                take_ph(h, 0, bank, h + 1, 0)

            def rgb_relu(r, ct, u, n, n_st):
                waits = []
                if ct == 0:
                    waits.append((win_loaded[u % 2], loads_seen(r, u, 0, 2, WIN_DMAS)))
                if n_st is None or n_st >= 2:
                    waits.append((f_ready, n - 1))
                for s, v in waits:
                    act.wait_ge(s, v)
                act.activation(f_relu[:, ct % 2, :], b_all[:, u % 2, ct, :, :].rearrange("p f c -> p (f c)"),
                               ACT.Relu, bias=gr_win[:, u % 2, ct, CI:GR]).then_inc(relu_done, 1)

            def exp(ct, n):
                act.wait_ge(max_lifted, n + 1)
                act.activation(probs[:, ct % RP, :], neg_s[:, ct % 2, :], ACT.Exp, bias=lifted[:, ct % 2:ct % 2 + 1],
                               scale=-1.0, accum_out=sums[:, ct:ct + 1]).then_inc(exp_done, 1)

            def take_t(par, n):
                act.wait_ge(t_done, n * 3 + 1)
                act.copy(p_t[:, par, 0:8, :], t_ps[0:KB, 0, :].rearrange("p (k q) -> p k q", q=P))
                act.wait_ge(t_done, n * 3 + 3)
                act.copy(p_t[:, par, 8:BLOCKS, :], t_ps[0:KB, 2, 0:2 * P].rearrange("p (k q) -> p k q", q=P))
                act.copy(p_t_low[:, par, 8:BLOCKS, :], t_ps[0:KB, 2, 2 * P:4 * P].bitcast(F16)
                         .rearrange("p (k q) -> p k q", q=P)).then_inc(t_act, 1)

            def take_yt(count):
                act.wait_ge(yt_done, count)
                act.copy(y_t[:, :], ma_ps[:, 0:3 * P]).then_inc(yt_copied, 1)

            def take_z(h, par, count, row):
                act.wait_ge(z_done, count)
                act.wait_ge(o_ready, row + 1)
                act.activation(z_row[:, par, :, h * 3 * TILE_COLS:(h + 1) * 3 * TILE_COLS]
                               .rearrange("p f (t c) -> p t f c", c=TILE_COLS),
                               ma_ps[:, 0:3 * P].rearrange("p (t f c) -> p t f c", f=F, c=TILE_COLS),
                               ACT.Identity, bias=B_OUT).then_inc(z_ready, 1)

            def step(r, u, r_st):
                slot = (u + LEAD) % RING
                back, ahead = r_st != 0, r_st != HEIGHT - 1
                more = r_st is None or r_st + LEAD < HEIGHT
                for ct in range(TILES):
                    n = r * TILES + ct
                    n_st = None if r_st is None else r_st * TILES + ct
                    if n_st is None or n_st >= 2:
                        take_t(ct % 2, n - 2)
                    if ct in (0, 4) and back:
                        take_yt(r * 2 - 1 + ct // 4)
                    if ct < 2 and more:
                        take_th(ct, slot, (r + LEAD) * 2 + (ct + 1))
                    exp(ct, n)
                    rgb_relu(r, ct, u, n, n_st)
                    if ct in (1, 5) and back:
                        take_z(ct // 4, (u + 1) % 2, r * 2 - 1 + ct // 4, r - 1)
                    if ct == 2 and ahead:
                        take_ph(0, (u + 1) % 2, ma_ps, r * 2 + 3, r + 1)
                    if ct == 4 and ahead:
                        take_ph(1, (u + 1) % 2, mb_ps, r * 2 + 4, r + 1)
                    if ct == 3 and more:
                        if back:
                            act.wait_ge(pv_done, r * TILES)
                        take_g_high(0, slot, (r + LEAD) * 2 + 1)
                    if ct == 5 and more:
                        take_g_high(1, slot, (r + LEAD) * 2 + 2)

            rows_loop(act, step)
            for n in (HEIGHT * TILES - 2, HEIGHT * TILES - 1):
                take_t(n % 2, n)
            for h in range(2):
                take_yt(2 * HEIGHT - 1 + h)
                take_z(h, 1, 2 * HEIGHT - 1 + h, HEIGHT - 1)

        @block.vector
        def _(dve):
            dve.memset(zeros[:, :], 0.0).then_inc(zeroed, 1)
            dve.memset(x_pad[:, :, :, :], 0.0).then_inc(zeroed, 1)
            dve.memset(th_lo[:, :, :, :].bitcast(F32), 0.0).then_inc(zeroed, 1)
            dve.memset(g_t[:, RING - 3:RING, :, :, :, :], 0.0).then_inc(zeroed, 1)
            dve.memset(factor[:, :, :], 1.0).then_inc(zeroed, 1)
            dve.wait_ge(consts, 16 * NCONST)
            dve.tensor_tensor(B_OUT, B_OUT, B_OUT_R, ALU.add).then_inc(w_ready, 1)
            dve.wait_ge(zeroed, 5)
            dve.wait_ge(w_ready, 8)
            dve.wait_ge(patched, 16 * 2 * HF)

            def low_th(h, slot, count):
                dve.wait_ge(th_high, count)
                dve.scalar_tensor_tensor(th_lo[:, bass.ds(slot, 1), h * HF:(h + 1) * HF, 3:3 + WIDTH]
                                         .rearrange("p a f c -> p (a f) c"),
                                         mb_ps[0:CI, 0:HALF].rearrange("p (f c) -> p f c", c=WIDTH), B_TH[0:CI],
                                         th_hi[0:CI, bass.ds(slot, 1), h * HF:(h + 1) * HF, 3:3 + WIDTH]
                                         .rearrange("p a f c -> p (a f) c").bitcast(F32),
                                         ALU.add, ALU.subtract).then_inc(th_ready, 1)

            def take_g(h, count):
                dve.wait_ge(g_done, count)
                dve.tensor_tensor(g_sum[:, h, :], mb_ps[0:KB, 0:6 * CI],
                                  g_bias[:, 3 * h:3 * h + 3, :, :].rearrange("p t h k -> p (t h k)"),
                                  ALU.add).then_inc(g_summed, 1)

            def take_g_low(h, slot, count):
                dve.wait_ge(g_rested, count)
                rest, cut = (t.rearrange("p (a k) -> p a k", k=CI) for t in (g_rest[:, h, :], high(g_rest[:, h, :])))
                dve.tensor_tensor(g_t[:, slot, 3 * h:3 * h + 3, :, 2, :].rearrange("p t h k -> p (t h) k"), rest, cut,
                                  ALU.subtract).then_inc(g_ready, 1)

            def low_ph(h, par, bank, count):
                dve.wait_ge(ph_high, count)
                for f in range(HF):
                    stt = dve.scalar_tensor_tensor(
                        ph_hl[CI:P, par, :, h * HF + f, :],
                        bank[0:CI, f * WIDTH:(f + 1) * WIDTH].rearrange("p (t c) -> p t c", c=TILE_COLS), B_PH[0:CI],
                        ph_hl[0:CI, par, :, h * HF + f, :].bitcast(F32), ALU.add, ALU.subtract)
                stt.then_inc(ph_ready, 1)

            def copy_windows(h, par, seen):
                wait_apart(dve, (zeroed, 5), [(pad_loaded[par], seen)])
                dve.tensor_copy(x_win[:, 3 * h:3 * h + 3, :, :].rearrange("p t h (f c) -> p t (h f) c", c=WIN),
                                row_windows(x_pad[:, par, :, 3 * h * TILE_COLS:], WIN, TILES // 2)
                                ).then_inc(win_copied, 1)

            for t in range(LEAD):
                for h in range(2):
                    copy_windows(h, t % 2, 16 * (t // 2 + 1))
                for h in range(2):
                    low_th(h, t, 2 * t + h + 1)
                for h in range(2):
                    take_g(h, 2 * t + h + 1)
                for h in range(2):
                    take_g_low(h, t, 2 * t + h + 1)
            for h, bank in enumerate((ma_ps, mb_ps)):
                low_ph(h, 0, bank, h + 1)

            def mask_scores(par, n):
                waits = [(s_done, n + 1)]
                if not (isinstance(n, int) and n < 2):
                    waits.append((exp_done, n - 1))
                wait_apart(dve, (zeroed, 5), waits)
                dve.tensor_tensor_reduce(neg_s[:, par, :].rearrange("p (b k) -> p b k", b=2), s_ps[:, :, 0:NKEYS // 2],
                                         mask[:, :].rearrange("p (b k) -> p b k", b=2), -1.0, BIG,
                                         ALU.add, ALU.min, neg_max[:, par:par + 1]).then_inc(s_masked, 1)
                dve.wait_ge(s_masked, n + 1)
                dve.tensor_scalar(lifted[:, par:par + 1], neg_max[:, par:par + 1], LIFT, None,
                                  ALU.add).then_inc(max_lifted, 1)

            def take_t(par, n):
                dve.wait_ge(t_done, n * 3 + 2)
                dve.tensor_copy(p_t_low[:, par, 0:8, :], t_ps[0:KB, 1, :].bitcast(F16)
                                .rearrange("p (k q) -> p k q", q=P)).then_inc(t_dve, 1)

            def divide(ct, n):
                dve.wait_ge(exp_done, n + 1)
                dve.reciprocal(factor[:, ct, 0:GP], sums[:, ct:ct + 1].broadcast_to([P, GP])).then_inc(inverted, 1)
                dve.wait_ge(inverted, n + 1)
                dve.wait_ge(pv_done, n + 1)
                dve.tensor_tensor(y_sb[:, ct, 0:GP + 1, :], y_ps[:, 0:(GP + 1) * CI].rearrange("p (a k) -> p a k", k=CI),
                                  factor[:, ct, :].rearrange("p (a o) -> p a o", o=1).broadcast_to([P, GP + 1, CI]),
                                  ALU.mult).then_inc(y_divided, 1)
                dve.wait_ge(y_divided, n + 1)
                dve.tensor_reduce(y_sb[:, ct, GP + 1, :], y_sb[:, ct, 0:GP, :].rearrange("p a k -> p k a"),
                                  AX.X, ALU.add).then_inc(y_ready, 1)

            def step(r, u, r_st):
                slot = (u + LEAD) % RING
                ahead = r_st != HEIGHT - 1
                more = r_st is None or r_st + LEAD < HEIGHT
                for ct in range(TILES):
                    n = r * TILES + ct
                    n_st = None if r_st is None else r_st * TILES + ct
                    mask_scores(ct % 2, n)
                    if n_st is None or n_st >= 2:
                        take_t(ct % 2, n - 2)
                    if ct < 2 and more:
                        low_th(ct, slot, (r + LEAD) * 2 + (ct + 1))
                        copy_windows(ct, u % 2, loads_seen(r, u, LEAD, 2))
                    if ct in (2, 3) and more:
                        take_g(ct - 2, (r + LEAD) * 2 + (ct - 1))
                    if ct in (3, 5) and ahead:
                        low_ph(ct // 5, (u + 1) % 2, (ma_ps, mb_ps)[ct // 5], r * 2 + (3 + ct // 5))
                    if ct in (4, 5) and more:
                        take_g_low(ct - 4, slot, (r + LEAD) * 2 + (ct - 3))
                    if n_st is None or n_st >= 3:
                        divide((ct - 3) % TILES, n - 3)
                    if ct == 2 and not more and ahead:
                        dve.memset(th_hi[:, slot, :, :].bitcast(F32), 0.0).then_inc(th_ready, 1)
                        dve.memset(th_lo[:, slot, :, :].bitcast(F32), 0.0).then_inc(th_ready, 1)
                        dve.memset(g_t[:, slot, :, :, :, :], 0.0).then_inc(g_ready, 2)

            rows_loop(dve, step)
            n = HEIGHT * TILES
            take_t(0, n - 2)
            divide(TILES - 3, n - 3)
            take_t(1, n - 1)
            divide(TILES - 2, n - 2)
            divide(TILES - 1, n - 1)

        @block.gpsimd
        def _(pool):
            pool.sem_inc(o_ready, 2)
            for u in range(2):
                pool.sem_inc(stored[u], 16)
            pool.memset(th_hi[:, :, :, :].bitcast(F32), 0.0).then_inc(th_zeroed, 1)
            pool.wait_ge(consts, 16 * NCONST)

            def rgb_weights(ct, u, n, n_st):
                pool.wait_ge(relu_done, n + 1)
                if n_st is None or n_st >= RF:
                    pool.wait_ge(pv_done, n + (1 - RF))
                pool.tensor_tensor(f_rgb[:, f_slot(ct, u), :], f_relu[:, ct % 2, :], rgb_mask[:, :],
                                   ALU.mult).then_inc(f_ready, 1)

            def low_parts(ct, n):
                pool.wait_ge(exp_done, n + 1)
                pool.tensor_tensor(probs_low[:, ct % RP, :], probs[:, ct % RP, :], high(probs[:, ct % RP, :]),
                                   ALU.subtract).then_inc(low_ready, 1)

            def rest_of_g(h, count):
                pool.wait_ge(g_summed, count)
                pool.tensor_tensor(g_rest[:, h, :], g_sum[:, h, :], high(g_sum[:, h, :]),
                                   ALU.subtract).then_inc(g_rested, 1)

            for t in range(LEAD):
                for h in range(2):
                    rest_of_g(h, 2 * t + h + 1)

            def residual(slot, par, row, seen):
                pool.wait_ge(z_ready, row * 2 + 2)
                pool.wait_ge(stored[par], seen)
                pool.tensor_tensor(o_row[:, par, :, :], z_row[:, par, :, :], x_row[:, slot, :, :],
                                   ALU.add).then_inc(o_ready, 1)

            def step(r, u, r_st):
                for ct in range(TILES):
                    n = r * TILES + ct
                    more = r_st is None or r_st + LEAD < HEIGHT
                    if ct in (3, 4) and more:
                        rest_of_g(ct - 3, (r + LEAD) * 2 + (ct - 2))
                    rgb_weights(ct, u, n, None if r_st is None else n)
                    low_parts(ct, r * TILES + ct)
                if r_st != 0:
                    residual((u - 1) % XR, (u - 1) % 2, r - 1, loads_seen(r, u, -1, 2))

            rows_loop(pool, step)
            residual(XR - 1, 1, HEIGHT - 1, 16 * ((HEIGHT - 1) // 2 + 1))


def layer1(nc, frames, x_dram, out_dram, g_w, g_b, theta_w, theta_b, phi_w, phi_b, W_w, W_b,
           bn_gamma, bn_beta, bn_mean, bn_var, identity_dram):
    nc.disable_value_cache = False
    CHUNKS = POS // QC
    GROUPS = CHUNKS // UNROLL
    KEYS = POS // 4
    KT = KEYS // P
    QT = QC // P
    CONV = 4 * WIDTH
    NCONV = POS // CONV
    SUB = 512
    SUBS = -(-KEYS // SUB)
    PARTS = QT * SUBS
    MX = 3
    KV_SLOTS = (14, 16)
    USES = PARTS + len(KV_SLOTS)
    START_USES = NCONV + PARTS
    FRAME_USES = CHUNKS * PARTS + NCONV
    POOLED = START_USES + UNROLL * PARTS + (CHUNKS - 2 * UNROLL) * USES
    V_SLOTS = (14, 15, 16, 17)
    PART_SLOTS = 13
    LO = CI + 1
    VW = LO + CI
    LAG = 4
    RING_P = 6
    POOL_LOW = 2
    LIFT = 12 * math.log(2.0)
    V_RANGE = 2.0 ** 11
    ROW_HI, ROW_LO = CI, CI + 32

    with ExitStack() as ctx:
        def sb(name, shape, dt=F32):
            return ctx.enter_context(nc.sbuf_tensor(name, shape, dt))

        def sem(name):
            return ctx.enter_context(nc.semaphore(name))

        x_sb = sb("x_sb", [P, 2, POS])
        w_nat = sb("w_nat", [P, 2, CH])
        wout_nat = sb("wout_nat", [P, CI])
        w_kv = sb("w_kv", [P, P])
        w_q = sb("w_q", [P, P])
        w_out_hi = sb("w_out_hi", [P, CH], F32R)
        w_out_lo = sb("w_out_lo", [CI, CH], F32R)
        ident = sb("ident1", [P, P])
        cols = sb("cols", [P, 12])
        B_Q, B_PHI, B_G, B_W, GAMMA, BETA, MEAN, VAR, STD, INV, OFFSET, EPS = (
            cols[:, n:n + 1] for n in range(12))
        kv_raw = sb("kv_raw", [P, KEYS])
        v_f32 = sb("v_f32", [CI, KEYS])
        v_max = sb("v_max", [CI, 2])
        v_scale = sb("v_scale", [CI, 1])
        v_unscale = sb("v_unscale", [CI, 1])
        v_unscale_next = sb("v_unscale_next", [CI, 1])
        lift = sb("lift", [1, 1])
        k_next = sb("k_next", [P, KEYS], F32R)
        k_hi = sb("k_hi", [P, KEYS], F32R)
        k_lo = sb("k_lo", [P, KEYS], F32R)
        v_t = sb("v_t", [P, KT, VW], F16)
        q_hl = sb("q_hl", [P, UNROLL, QC], F32R)
        q_mx = sb("q_mx", [P, UNROLL, QC], F32R)
        part_max = sb("part_max", [P, PARTS])
        neg_max = sb("neg_max", [P, QT])
        probs = sb("probs", [P, RING_P, QC])
        probs_low = sb("probs_low", [P, RING_P, QC], F16)
        o_sb = sb("o_sb", [P, QT, CI])
        o_rec = sb("o_rec", [P, QT])
        y_sb = sb("y_sb", [P, QT, CI])
        y_hl = sb("y_hl", [P, QC], F32R)
        z_sb = sb("z_sb", [P, UNROLL, QC])
        res = sb("res", [P, UNROLL, QC])

        mx_ps = ctx.enter_context(nc.psum_tensor("mx_ps", [P, MX, 512], F32))
        st_ps = ctx.enter_context(nc.psum_tensor("st_ps", [P, 2, 512], F32))
        o_ps = ctx.enter_context(nc.psum_tensor("o_ps", [P, 2, 512], F32))
        m_ps = ctx.enter_context(nc.psum_tensor("m_ps", [P, 512], F32))

        consts_loaded = sem("consts_loaded")
        zeroed = sem("zeroed")
        consts_ready = sem("consts_ready")
        std_ready = sem("std_ready")
        w_turned = sem("w_turned")
        w_ready = sem("w_ready")
        x_loaded = sem("x_loaded")
        knext_ready = sem("knext_ready")
        khi_ready = sem("khi_ready")
        klo_ready = sem("klo_ready")
        v_biased = sem("v_biased")
        v_bounded = sem("v_bounded")
        v_factored = sem("v_factored")
        v_scaled = sem("v_scaled")
        v_high = sem("v_high")
        v_turned = sem("v_turned")
        v_ready = sem("v_ready")
        q_done = sem("q_done")
        q_copied = sem("q_copied")
        q_low = sem("q_low")
        mx_done = sem("mx_done")
        mx_reduced = sem("mx_reduced")
        max_ready = sem("max_ready")
        maxrow_done = sem("maxrow_done")
        maxrow_high = sem("maxrow_high")
        maxrow_low = sem("maxrow_low")
        st_done = sem("st_done")
        exp_done = sem("exp_done")
        low_pool = sem("low_pool")
        low_dve = sem("low_dve")
        pv_done = sem("pv_done")
        o_low = sem("o_low")
        o_copied = sem("o_copied")
        y_ready = sem("y_ready")
        yt_done = sem("yt_done")
        yt_copied = sem("yt_copied")
        yt_low = sem("yt_low")
        z_done = sem("z_done")
        z_ready = sem("z_ready")
        res_ready = sem("res_ready")
        stored = [sem(f"stored{u}") for u in range(UNROLL)]

        XLOADS = 4
        PER = POS // XLOADS
        CREDIT = UNROLL

        def prob_high(kt):
            return probs[:, kt % RING_P, :].bitcast(BF16).rearrange("p (n half) -> p n half", half=2)[:, :, 1]

        def parts_of(kt):
            return range(min(kt, PART_SLOTS) * PARTS // PART_SLOTS, min(kt + 1, PART_SLOTS) * PARTS // PART_SLOTS)

        def uses_before(b, i, u):
            if isinstance(i, int):
                at = START_USES + i * PARTS + (NCONV if i >= UNROLL else 0)
                return b * FRAME_USES + at, at
            at = START_USES + UNROLL * (PARTS - USES) + u * USES
            return b * FRAME_USES + chunk_group[0] * (UNROLL * USES) + at, at

        chunk_group = [None]

        def by_pool(kt):
            return kt % 3 < POOL_LOW

        def low_parts(eng, kt, g, done):
            eng.wait_ge(exp_done, g * KT + (kt + 1))
            eng.tensor_tensor(probs_low[:, kt % RING_P, :], probs[:, kt % RING_P, :], prob_high(kt),
                              ALU.subtract).then_inc(done, 1)

        def chunk_loop(eng, chunk):
            chunk.start()
            with eng.Fori(0, frames) as b:
                for u in range(UNROLL):
                    chunk(b, b * CHUNKS + u, u, u, u == 0, False)
                with eng.Fori(1, GROUPS - 1) as it:
                    chunk_group[0] = it
                    for u in range(UNROLL):
                        chunk(b, b * CHUNKS + it * UNROLL + u, it * UNROLL + u, u, False, False)
                for u in range(UNROLL):
                    i = CHUNKS - UNROLL + u
                    chunk(b, b * CHUNKS + i, i, u, False, i)
                chunk.end(b)

        block = ctx.enter_context(nc.Block())

        @block.sync
        def _(sp):
            for n, w in enumerate((phi_w, g_w)):
                sp.dma_start(w_nat[n * CI:(n + 1) * CI, 0, :], w).then_inc(consts_loaded, 16)
                sp.dma_start(w_nat[n * CI:(n + 1) * CI, 1, :], theta_w).then_inc(consts_loaded, 16)
                sp.dma_start(B_Q[n * CI:(n + 1) * CI], column(theta_b)).then_inc(consts_loaded, 16)
            sp.dma_start(wout_nat[:, :], W_w).then_inc(consts_loaded, 16)
            sp.dma_start(ident[:, :], identity_dram).then_inc(consts_loaded, 16)
            sp.dma_start(B_PHI[0:CI], column(phi_b)).then_inc(consts_loaded, 16)
            sp.dma_start(B_G[CI:P], column(g_b)).then_inc(consts_loaded, 16)
            for dst, src in ((B_W, W_b), (GAMMA, bn_gamma), (BETA, bn_beta), (MEAN, bn_mean), (VAR, bn_var)):
                sp.dma_start(dst, column(src)).then_inc(consts_loaded, 16)

            def load(b, slot):
                for n in range(XLOADS):
                    sp.dma_start(x_sb[:, bass.ds(slot, 1), n * PER:(n + 1) * PER],
                                 x_dram[bass.ds(b, 1), :, n * PER:(n + 1) * PER].rearrange("a c n -> c a n")
                                 ).then_inc(x_loaded, 16)

            def stores(b):
                with sp.Fori(0, GROUPS) as it:
                    for u in range(UNROLL):
                        g = b * CHUNKS + it * UNROLL + u
                        sp.wait_ge(res_ready, g + 1 + CREDIT)
                        sp.dma_start(out_dram[bass.ds(b, 1), :, bass.ds(it * (UNROLL * QC) + u * QC, QC)]
                                     .rearrange("a c n -> c (a n)"), res[:, u, :]).then_inc(stored[u], 16)

            load(0, 0)
            sp.wait_ge(x_loaded, 16 * XLOADS)
            load(1, 1)
            if frames > 2:
                with sp.Fori(0, frames - 2) as b:
                    stores(b)
                    sp.wait_ge(res_ready, (b + 1) * CHUNKS + CREDIT)
                    sp.wait_ge(x_loaded, (b + 2) * (16 * XLOADS))
                    load(b + 2, b % 2)
            sp.wait_ge(x_loaded, frames * (16 * XLOADS))
            sp.sem_inc(x_loaded, 16 * XLOADS)
            with sp.Fori(frames - 2, frames) as b:
                stores(b)
            for u in range(UNROLL):
                sp.wait_ge(stored[u], 16 * (frames * GROUPS + 1))

        @block.gpsimd
        def _(pool):
            pool.sem_inc(res_ready, CREDIT)
            for u in range(UNROLL):
                pool.sem_inc(stored[u], 16)

            def residual(b, g, i, u):
                pool.wait_ge(z_ready, g + 2)
                pool.wait_ge(stored[u], (b * GROUPS + i // UNROLL + 1) * 16 if isinstance(i, int)
                             else (b * GROUPS + i[0] + 1) * 16)
                pool.tensor_tensor(res[:, u, :], z_sb[:, u, :],
                                   x_sb[:, bass.ds(b % 2, 1), bass.ds(i * QC if isinstance(i, int)
                                                                      else i[0] * (UNROLL * QC) + i[1] * QC, QC)]
                                   .rearrange("p a n -> p (a n)"), ALU.add).then_inc(res_ready, 1)

            def chunk(b, g, i, u, first, last):
                before = (u + UNROLL - 1) % UNROLL
                for kt in range(KT):
                    if by_pool(kt):
                        low_parts(pool, kt, g, low_pool)
                    if kt == 10 and not first:
                        residual(b, g - 1, chunk.before(i, u), before)

            def end(b):
                residual(b, (b + 1) * CHUNKS - 1, CHUNKS - 1, UNROLL - 1)

            def before(i, u):
                if isinstance(i, int):
                    return i - 1
                return (chunk_group[0] - 1, UNROLL - 1) if u == 0 else (chunk_group[0], u - 1)

            chunk.start, chunk.end, chunk.before = lambda: None, end, before
            chunk_loop(pool, chunk)

        @block.tensor
        def _(pe):
            pe.wait_ge(consts_loaded, 16 * 15)
            pe.transpose(m_ps[:, 0:P], w_nat[:, 0, :], ident[:, :]).then_inc(w_turned, 1)
            pe.transpose(m_ps[:, P:2 * P], w_nat[:, 1, :], ident[:, :]).then_inc(w_turned, 1)
            pe.transpose(m_ps[0:CI, 2 * P:3 * P], wout_nat[:, :], ident[:, :]).then_inc(w_turned, 1)
            pe.wait_ge(w_ready, 5)
            pe.wait_ge(zeroed, 7)

            def conv_q(slot, j, u):
                pe.matmul(m_ps[:, :], w_q[:, :],
                          x_sb[:, bass.ds(slot, 1), bass.ds(j * QC, QC)].rearrange("p a n -> p (a n)"),
                          start=True, stop=True).then_inc(q_done, 1)

            def max_scores(u, part, use, at, keys):
                pe.wait_ge(mx_reduced, use + (1 - MX))
                key = (part % SUBS) * SUB
                width = min(SUB, KEYS - key)
                pe.matmul(mx_ps[:, at % MX, 0:width], q_hl[:, u, (part // SUBS) * P:(part // SUBS + 1) * P],
                          keys[:, key:key + width], start=True, stop=True).then_inc(mx_done, 1)

            def conv_kv(slot, column, use, at):
                if use is not None:
                    pe.wait_ge(mx_reduced, use + (1 - MX))
                pe.matmul(mx_ps[:, at % MX, 0:CONV], w_kv[:, :],
                          x_sb[:, bass.ds(slot, 1), bass.ds(column, CONV)].rearrange("p a n -> p (a n)"),
                          start=True, stop=True).then_inc(mx_done, 1)

            def turn_v(tiles):
                for kt in tiles:
                    tr = pe.transpose(mx_ps[:, kt // 8, (kt % 8) * CI:(kt % 8 + 1) * CI],
                                      v_f32[:, kt * P:(kt + 1) * P], ident[0:CI, 0:CI])
                if tiles[-1] == KT - 1:
                    tr.then_inc(v_turned, 1)

            def max_row(g):
                pe.wait_ge(max_ready, g + 1)
                for q in range(QT):
                    mm = pe.transpose(m_ps[0:1, q * P:(q + 1) * P], neg_max[:, q:q + 1], ident[:, :])
                mm.then_inc(maxrow_done, 1)

            def scores(u, kt):
                pe.matmul(st_ps[:, kt % 2, :], k_hi[:, kt * P:(kt + 1) * P], q_hl[:, u, :],
                          start=True, stop=False)
                pe.matmul(st_ps[:, kt % 2, :], k_lo[:, kt * P:(kt + 1) * P], q_mx[:, u, :],
                          start=False, stop=True).then_inc(st_done, 1)

            def values(kt, g):
                if by_pool(kt):
                    pe.wait_ge(low_pool, g * (KT * POOL_LOW // 3) + (kt // 3 * POOL_LOW + kt % 3 + 1))
                else:
                    pe.wait_ge(low_dve, g * (KT * (3 - POOL_LOW) // 3)
                               + (kt // 3 * (3 - POOL_LOW) + kt % 3 - POOL_LOW + 1))
                for q in range(QT):
                    o = o_ps[:, q // 2, (q % 2) * VW:(q % 2 + 1) * VW]
                    pairs = [(o, prob_high(kt), v_t[:, kt, :]),
                             (o[:, 0:LO], probs_low[:, kt % RING_P, :], v_t[:, kt, 0:LO])]
                    for n, (out, part, v) in enumerate(pairs if q < QT - 1 else pairs[::-1]):
                        mm = pe.matmul(out, part[:, q * P:(q + 1) * P], v,
                                       start=(kt == 0 and q % 2 == 0 and n == 0), stop=(kt == KT - 1 and n == 1),
                                       skip_group_check=True)
                mm.then_inc(pv_done, 1)

            def turn_y(g, more=()):
                wait_apart(pe, (zeroed, 7), [(y_ready, g + 1), *more])
                for q in range(QT):
                    mm = pe.transpose(m_ps[0:CI, q * P:(q + 1) * P], y_sb[:, q, :], ident[:, :])
                mm.then_inc(yt_done, 1)

            def conv_out(g):
                pe.wait_ge(yt_low, g + 1)
                pe.matmul(m_ps[:, :], w_out_hi[:, :], y_hl[:, :], start=True, stop=False)
                pe.matmul(m_ps[:, :], w_out_lo[:, :], y_hl[0:CI, :], start=False, stop=True).then_inc(z_done, 1)

            def chunk(b, g, i, u, first, last):
                static = isinstance(last, bool)
                i_st = i if not static else None
                uses, at = uses_before(b, i, u)
                used = 0
                for kt in range(KT):
                    if kt == 0:
                        pe.wait_ge(maxrow_low, g + 1)
                        if first:
                            pe.wait_ge(khi_ready, b + 1)
                            pe.wait_ge(klo_ready, b + 1)
                    if not (first and kt < 2):
                        pe.wait_ge(exp_done, g * KT + (kt - 1))
                    scores(u, kt)
                    if kt == 0:
                        pe.wait_ge(q_low, g + 2)
                        if first:
                            pe.wait_ge(v_ready, b + 1)
                        if i_st == CHUNKS - 1:
                            pe.wait_ge(knext_ready, (b + 2) * 4)
                    for part in parts_of(kt):
                        max_scores((u + 1) % UNROLL, part, uses + used, at + used,
                                   k_next if i_st == CHUNKS - 1 else k_hi)
                        used += 1
                    if not isinstance(i, int) and kt in KV_SLOTS:
                        if u == 0:
                            pe.wait_ge(x_loaded, (b + 2) * (16 * XLOADS))
                        n = u * len(KV_SLOTS) + KV_SLOTS.index(kt)
                        per_group = UNROLL * len(KV_SLOTS)
                        conv_kv((b + 1) % 2, (chunk_group[0] - 1) * (per_group * CONV) + n * CONV,
                                uses + used, at + used)
                        used += 1
                    if i_st == CHUNKS - 1 and kt in V_SLOTS:
                        wait_apart(pe, (zeroed, 7), [(mx_reduced, uses + PARTS), (v_scaled, (b + 2) * 2)])
                        n = V_SLOTS.index(kt)
                        turn_v(range(n * KT // len(V_SLOTS), (n + 1) * KT // len(V_SLOTS)))
                    if kt < LAG:
                        if not first:
                            values(KT - LAG + kt, g - 1)
                    elif kt == LAG + 1:
                        if not first:
                            pe.wait_ge(o_copied, g * 2)
                        values(0, g)
                        values(1, g)
                    elif kt > LAG:
                        values(kt - LAG, g)
                    if kt == 7 and not first:
                        turn_y(g - 1)
                    if kt == 9 and not first:
                        conv_out(g - 1)
                    if kt == 11:
                        if not first:
                            pe.wait_ge(z_ready, g + 1)
                        else:
                            pe.wait_ge(maxrow_low, g + 1)
                        if i_st is None or i_st + 2 < CHUNKS:
                            conv_q(b % 2, i + 2, (u + 2) % UNROLL)
                        else:
                            conv_q((b + 1) % 2, i_st + 2 - CHUNKS, (u + 2) % UNROLL)
                    if kt == 15:
                        pe.wait_ge(q_copied, g + 3)
                        pe.wait_ge(q_low, g + 3)
                        max_row(g + 1)

            def start():
                pe.wait_ge(x_loaded, 16 * XLOADS)
                for n in range(NCONV):
                    conv_kv(0, n * CONV, n if n >= MX else None, n)
                conv_q(0, 0, 0)
                pe.wait_ge(mx_reduced, NCONV)
                pe.wait_ge(v_scaled, 2)
                turn_v(range(KT))
                pe.wait_ge(q_copied, 1)
                pe.wait_ge(q_low, 1)
                conv_q(0, 1, 1)
                pe.wait_ge(knext_ready, 4)
                pe.wait_ge(v_ready, 1)
                for part in range(PARTS):
                    max_scores(0, part, NCONV + part, NCONV + part, k_next)
                pe.wait_ge(q_copied, 2)
                pe.wait_ge(q_low, 2)
                max_row(0)

            def end(b):
                g = (b + 1) * CHUNKS - 1
                for kt in range(KT - LAG, KT):
                    values(kt, g)
                turn_y(g, [(maxrow_low, g + 2)])
                conv_out(g)

            chunk.start, chunk.end = start, end
            chunk_loop(pe, chunk)

        @block.scalar
        def _(act):
            act.sem_inc(z_ready, 1)
            act.wait_ge(consts_loaded, 16 * 15)
            act.wait_ge(zeroed, 7)
            act.activation(STD, VAR, ACT.Sqrt, bias=EPS).then_inc(std_ready, 1)
            act.wait_ge(w_turned, 3)
            act.copy(w_kv[:, :], m_ps[:, 0:P]).then_inc(w_ready, 1)
            act.copy(w_q[:, :], m_ps[:, P:2 * P]).then_inc(w_ready, 1)
            act.copy(w_out_hi[0:CI, :], m_ps[0:CI, 2 * P:3 * P]).then_inc(w_ready, 1)
            act.copy(w_out_hi[CI:P, :], m_ps[0:CI, 2 * P:3 * P]).then_inc(w_ready, 1)
            act.wait_ge(consts_ready, 4)

            def take_q(u, g):
                act.wait_ge(q_done, g + 1)
                act.activation(q_hl[:, u, :], m_ps[:, :], ACT.Identity, bias=B_Q)
                act.activation(q_mx[0:CI, u, :], m_ps[0:CI, :], ACT.Identity, bias=B_Q[0:CI]).then_inc(q_copied, 1)

            def take_max(u, g):
                act.wait_ge(maxrow_done, g + 1)
                act.activation(q_mx[ROW_HI:ROW_HI + 1, u, :], m_ps[0:1, :], ACT.Identity,
                               bias=lift[:, :]).then_inc(maxrow_high, 1)

            def take_y(g):
                act.wait_ge(yt_done, g + 1)
                act.activation(y_hl[0:CI, :], m_ps[0:CI, :], ACT.Copy, scale=v_unscale[:, :]).then_inc(yt_copied, 1)

            def take_z(u, g):
                act.wait_ge(z_done, g + 1)
                act.wait_ge(res_ready, g + 1)
                act.activation(z_sb[:, u, :], m_ps[:, :], ACT.Identity, bias=OFFSET, scale=INV).then_inc(z_ready, 1)

            def chunk(b, g, i, u, first, last):
                i_st = None if isinstance(last, bool) else i
                before = (u + UNROLL - 1) % UNROLL
                for kt in range(KT):
                    act.wait_ge(st_done, g * KT + (kt + 1))
                    if not (first and kt < RING_P):
                        act.wait_ge(pv_done, g * KT + (kt + 1 - RING_P))
                    act.activation(probs[:, kt % RING_P, :], st_ps[:, kt % 2, :], ACT.Exp).then_inc(exp_done, 1)
                    if kt == 7 and not first:
                        take_y(g - 1)
                    if kt == 9 and not first:
                        take_z(before, g - 1)
                    if kt == 11:
                        take_q((u + 2) % UNROLL, g + 2)
                    if kt == 15:
                        take_max((u + 1) % UNROLL, g + 1)
                    if i_st in (CHUNKS - 3, CHUNKS - 2) and kt in (2, 5):
                        next_keys(2 * (i_st - (CHUNKS - 3)) + kt // 5, b * FRAME_USES + POOLED)
                    if i_st == CHUNKS - 1 and kt in (2, 5):
                        scale_v(kt // 5, b + 2)

            def next_keys(n, pooled):
                lo, hi = (0, CI) if n % 2 == 0 else (CI, P)
                some = slice(n // 2 * (KEYS // 2), (n // 2 + 1) * (KEYS // 2))
                act.wait_ge(mx_reduced, pooled)
                act.activation(k_next[lo:hi, some], kv_raw[0:CI, some], ACT.Identity,
                               bias=B_PHI[0:CI]).then_inc(knext_ready, 1)

            def scale_v(n, count):
                some = slice(n * (KEYS // 2), (n + 1) * (KEYS // 2))
                act.wait_ge(v_factored, count)
                act.activation(v_f32[:, some], v_f32[:, some], ACT.Copy, scale=v_scale[:, :]).then_inc(v_scaled, 1)

            def take_keys(count):
                act.wait_ge(knext_ready, count * 4)
                act.copy(k_hi[:, :], k_next[:, :].bitcast(F32)).then_inc(khi_ready, 1)

            def take_v(count):
                act.wait_ge(v_turned, count)
                for n in range(3):
                    tiles = min(8, KT - 8 * n)
                    act.copy(v_t[:, 8 * n:8 * n + tiles, 0:CI],
                             mx_ps[:, n, 0:tiles * CI].rearrange("p (t c) -> p t c", c=CI)).then_inc(v_high, 1)

            def start():
                for n in range(4):
                    next_keys(n, NCONV)
                take_q(0, 0)
                for n in range(2):
                    scale_v(n, 1)
                take_keys(1)
                take_v(1)
                act.copy(v_unscale[:, :], v_unscale_next[:, :])
                take_q(1, 1)
                take_max(0, 0)

            def end(b):
                g = (b + 1) * CHUNKS - 1
                take_keys(b + 2)
                act.wait_ge(pv_done, (b + 1) * (CHUNKS * KT))
                take_v(b + 2)
                take_y(g)
                act.wait_ge(yt_low, g + 1)
                act.copy(v_unscale[:, :], v_unscale_next[:, :])
                take_z(UNROLL - 1, g)

            chunk.start, chunk.end = start, end
            chunk_loop(act, chunk)

        @block.vector
        def _(dve):
            dve.memset(EPS, 1e-5).then_inc(zeroed, 1)
            dve.memset(lift[:, :], LIFT).then_inc(zeroed, 1)
            dve.memset(q_mx[CI:P, :, :].bitcast(F32), 0.0).then_inc(zeroed, 1)
            dve.memset(v_t[:, :, :], 1.0).then_inc(zeroed, 1)
            dve.memset(k_lo[CI:P, :].bitcast(F32), 0.0).then_inc(zeroed, 1)
            dve.wait_ge(zeroed, 5)
            dve.memset(k_lo[ROW_HI:ROW_HI + 1, :].bitcast(F32), 1.0).then_inc(zeroed, 1)
            dve.memset(k_lo[ROW_LO:ROW_LO + 1, :].bitcast(F32), 1.0).then_inc(zeroed, 1)
            dve.wait_ge(w_ready, 4)
            dve.tensor_tensor(w_out_lo[:, :], m_ps[0:CI, 2 * P:3 * P], w_out_hi[0:CI, :].bitcast(F32),
                              ALU.subtract).then_inc(w_ready, 1)
            dve.wait_ge(std_ready, 1)
            dve.reciprocal(INV, STD).then_inc(consts_ready, 1)
            dve.wait_ge(consts_ready, 1)
            dve.tensor_tensor(INV, INV, GAMMA, ALU.mult).then_inc(consts_ready, 1)
            dve.tensor_tensor(OFFSET, B_W, MEAN, ALU.subtract).then_inc(consts_ready, 1)
            dve.wait_ge(consts_ready, 3)
            dve.scalar_tensor_tensor(OFFSET, OFFSET, INV, BETA, ALU.mult, ALU.add).then_inc(consts_ready, 1)

            def pool_kv(column, use, at):
                dve.wait_ge(mx_done, use + 1)
                dve.tensor_reduce(kv_raw[:, bass.ds(column, CONV // 4)],
                                  mx_ps[:, at % MX, 0:CONV].rearrange("p (i r j c) -> p i j r c", r=2, c=2, j=WIDTH // 2),
                                  AX.XY, ALU.max).then_inc(mx_reduced, 1)

            def low_q(u, g):
                dve.wait_ge(q_copied, g + 1)
                dve.scalar_tensor_tensor(q_hl[CI:P, u, :], m_ps[CI:P, :], B_Q[CI:P],
                                         q_hl[CI:P, u, :].bitcast(F32), ALU.add, ALU.subtract).then_inc(q_low, 1)

            def reduce_max(part, use, at):
                dve.wait_ge(mx_done, use + 1)
                dve.tensor_reduce(part_max[:, part:part + 1], mx_ps[:, at % MX, 0:min(SUB, KEYS - part % SUBS * SUB)],
                                  AX.X, ALU.max).then_inc(mx_reduced, 1)

            def finish_max(uses):
                dve.wait_ge(mx_reduced, uses)
                dve.tensor_reduce(neg_max[:, :], part_max[:, :].rearrange("p (q s) -> p q s", s=SUBS),
                                  AX.X, ALU.max, negate=True).then_inc(max_ready, 1)

            def low_max(u, g):
                dve.wait_ge(maxrow_high, g + 1)
                dve.scalar_tensor_tensor(q_mx[ROW_LO:ROW_LO + 1, u, :], m_ps[0:1, :], LIFT,
                                         q_mx[ROW_HI:ROW_HI + 1, u, :].bitcast(F32),
                                         ALU.add, ALU.subtract).then_inc(maxrow_low, 1)

            def divide(g):
                dve.wait_ge(pv_done, (g + 1) * KT)
                o = o_ps[:, :, 0:2 * VW].rearrange("p bank (q v) -> p bank q v", v=VW)
                dve.tensor_copy(o_sb[:, :, :].rearrange("p (bank q) c -> p bank q c", q=2),
                                o[:, :, :, LO:VW]).then_inc(o_low, 1)
                dve.reciprocal(o_rec[:, :].rearrange("p (bank q) -> p bank q", q=2),
                               o[:, :, :, CI]).then_inc(o_copied, 1)
                dve.wait_ge(o_low, g + 1)
                dve.tensor_tensor(o_sb[:, :, :].rearrange("p (bank q) c -> p bank q c", q=2),
                                  o_sb[:, :, :].rearrange("p (bank q) c -> p bank q c", q=2),
                                  o[:, :, :, 0:CI], ALU.add).then_inc(o_copied, 1)
                dve.wait_ge(o_copied, (g + 1) * 2)
                dve.tensor_tensor(y_sb[:, :, :], o_sb[:, :, :],
                                  o_rec[:, :].rearrange("p (q a) -> p q a", a=1).broadcast_to([P, QT, CI]),
                                  ALU.mult).then_inc(y_ready, 1)

            def low_y(g):
                dve.wait_ge(yt_copied, g + 1)
                dve.scalar_tensor_tensor(y_hl[CI:P, :], m_ps[0:CI, :], v_unscale[:, :], y_hl[0:CI, :].bitcast(F32),
                                         ALU.mult, ALU.subtract).then_inc(yt_low, 1)

            def bias_v(pooled):
                dve.wait_ge(mx_reduced, pooled)
                dve.tensor_scalar(v_f32[:, :], kv_raw[CI:P, :], B_G[CI:P], None, ALU.add).then_inc(v_biased, 1)

            def bound_v(n, count):
                dve.wait_ge(v_biased, count)
                dve.tensor_reduce(v_max[:, n:n + 1], v_f32[:, n * (KEYS // 2):(n + 1) * (KEYS // 2)], AX.X, ALU.max,
                                  apply_absolute_value=True).then_inc(v_bounded, 1)

            def factor_v(count):
                dve.wait_ge(v_bounded, count * 4 - 2)
                dve.tensor_tensor(v_max[:, 0:1], v_max[:, 0:1], v_max[:, 1:2], ALU.max).then_inc(v_bounded, 1)
                dve.wait_ge(v_bounded, count * 4 - 1)
                dve.tensor_scalar(v_unscale_next[:, :], v_max[:, 0:1], 1e-30, 1.0 / V_RANGE,
                                  ALU.max, ALU.mult).then_inc(v_bounded, 1)
                dve.wait_ge(v_bounded, count * 4)
                dve.reciprocal(v_scale[:, :], v_unscale_next[:, :]).then_inc(v_factored, 1)

            def low_keys(count):
                dve.wait_ge(knext_ready, count * 4)
                dve.scalar_tensor_tensor(k_lo[0:CI, :], kv_raw[0:CI, :], B_PHI[0:CI],
                                         k_next[0:CI, :].bitcast(F32), ALU.add, ALU.subtract).then_inc(klo_ready, 1)

            def low_v(count):
                for n in range(3):
                    tiles = min(8, KT - 8 * n)
                    dve.wait_ge(v_high, count * 3 + (n - 2))
                    low = dve.tensor_tensor(v_t[:, 8 * n:8 * n + tiles, LO:VW],
                                            mx_ps[:, n, 0:tiles * CI].rearrange("p (t c) -> p t c", c=CI),
                                            v_t[:, 8 * n:8 * n + tiles, 0:CI], ALU.subtract)
                low.then_inc(v_ready, 1)

            def chunk(b, g, i, u, first, last):
                i_st = None if isinstance(last, bool) else i
                uses, at = uses_before(b, i, u)
                used = 0
                for kt in range(KT + 1):
                    if kt == LAG - 0 and not first:
                        divide(g - 1)
                    if kt > 0 and not by_pool(kt - 1):
                        low_parts(dve, kt - 1, g, low_dve)
                    if kt < KT:
                        for part in parts_of(kt):
                            reduce_max(part, uses + used, at + used)
                            used += 1
                    if kt == 8 and not first:
                        low_y(g - 1)
                    if kt == 12:
                        low_q((u + 2) % UNROLL, g + 2)
                    if kt == 13:
                        finish_max(uses + PARTS)
                    if kt == 16:
                        low_max((u + 1) % UNROLL, g + 1)
                    if not isinstance(i, int) and kt in KV_SLOTS:
                        n = u * len(KV_SLOTS) + KV_SLOTS.index(kt)
                        per_group = UNROLL * len(KV_SLOTS)
                        pool_kv((chunk_group[0] - 1) * (per_group * CONV // 4) + n * (CONV // 4), uses + used, at + used)
                        used += 1
                    if i_st == CHUNKS - 3 and kt == 14:
                        bias_v(uses + PARTS)
                    if i_st == CHUNKS - 3 and kt == 17:
                        bound_v(0, b + 2)
                    if i_st == CHUNKS - 2 and kt == 14:
                        bound_v(1, b + 2)
                    if i_st == CHUNKS - 2 and kt == 17:
                        factor_v(b + 2)

            def start():
                for n in range(NCONV):
                    pool_kv(n * (CONV // 4), n, n)
                dve.wait_ge(mx_reduced, NCONV)
                bias_v(NCONV)
                for n in range(2):
                    bound_v(n, 1)
                factor_v(1)
                low_keys(1)
                low_q(0, 0)
                low_v(1)
                low_q(1, 1)
                for part in range(PARTS):
                    reduce_max(part, NCONV + part, NCONV + part)
                finish_max(START_USES)
                low_max(0, 0)

            def end(b):
                dve.wait_ge(st_done, (b + 1) * (CHUNKS * KT))
                low_keys(b + 2)
                divide((b + 1) * CHUNKS - 1)
                low_v(b + 2)
                low_y((b + 1) * CHUNKS - 1)

            chunk.start, chunk.end = start, end
            chunk_loop(dve, chunk)


def program(nc, a, ident, mask, rgb_mask, out):
    gr = nc.dram_tensor("rgb_fields_padded", (PW, PW, GR), F32).ap()
    x1 = nc.dram_tensor("layer0_out", (FRAMES, CH, HEIGHT, WIDTH), F32).ap()
    p = "L0_conv_"
    nc.disable_value_cache = True
    rgb_fields(nc, a[p + "rgb"].rearrange("o c h w -> (o c) h w"), a[p + "rgb_g_w"], a[p + "rgb_g_b"],
               a[p + "rgb_theta_w"], a[p + "rgb_theta_b"], a[p + "cp_w"], ident, gr)
    layer0(nc, a["x"], gr, x1, ident, mask, rgb_mask,
           *(a[p + n] for n in ("g_w", "g_b", "theta_w", "theta_b", "phi_w", "phi_b", "W_w", "W_b",
                                "rgb_phi_w", "rgb_phi_b", "rgb_W_w", "rgb_W_b", "cp_w")))
    p = "L1_conv_"
    layer1(nc, FRAMES, x1.rearrange("f c h w -> f c (h w)"), out.rearrange("f c h w -> f c (h w)"),
           *(a[p + n] for n in ("g_w", "g_b", "theta_w", "theta_b", "phi_w", "phi_b", "W_w", "W_b",
                                "bn_gamma", "bn_beta", "bn_mean", "bn_var")), ident)


def neighbour_mask(order, frames, inside, outside):
    taps = {-3: (-3, 0, 3), -1: (-1, 0, 1), 0: (-3, -1, 0, 1, 3), 1: (-1, 0, 1), 3: (-3, 0, 3)}
    one = np.full((TILE_COLS, len(order), frames, TILE_COLS + 6), outside, np.float32)
    for q in range(TILE_COLS):
        for j, dy in enumerate(order):
            for dx in taps[dy]:
                one[q, j, :, q + 3 + dx] = inside
    return np.tile(one.reshape(TILE_COLS, -1), (FRAMES, 1))


_L0 = ["rgb", "g_w", "g_b", "theta_w", "theta_b", "phi_w", "phi_b", "W_w", "W_b", "rgb_g_w", "rgb_g_b",
       "rgb_theta_w", "rgb_theta_b", "rgb_phi_w", "rgb_phi_b", "rgb_W_w", "rgb_W_b", "cp_w"]
_L1 = ["g_w", "g_b", "theta_w", "theta_b", "phi_w", "phi_b", "W_w", "W_b",
       "bn_gamma", "bn_beta", "bn_mean", "bn_var"]
_INS = ["x"] + ["L0_conv_" + n for n in _L0] + ["L1_conv_" + n for n in _L1]


def kernel(**inputs):
    import concourse.bacc as _bacc
    from concourse.bass_utils import run_bass_kernel_spmd as _run

    nc = _bacc.Bacc("TRN2", target_bir_lowering=False, num_devices=1)
    arrays, aps = {}, {}

    def given(name, array):
        arrays[f"in_{name}_dram"] = array
        return nc.dram_tensor(f"in_{name}_dram", array.shape, mybir.dt.from_np(array.dtype),
                              kind="ExternalInput").ap()

    for name in _INS:
        aps[name] = given(name, np.ascontiguousarray(inputs[name]))
    ident = given("identity", np.eye(P, dtype=np.float32))
    mask = given("mask", neighbour_mask(ROWS, FRAMES, 0.0, -1.0e30))
    rgb_mask = given("rgb_mask", np.ascontiguousarray(neighbour_mask(sorted(ROWS), 1, 1.0, 0.0).T))
    out = nc.dram_tensor("out_0_dram", (FRAMES, CH, HEIGHT, WIDTH), F32, kind="ExternalOutput").ap()
    program(nc, aps, ident, mask, rgb_mask, out)
    r = _run(nc, [arrays], core_ids=[0])
    return r.results[0]["out_0_dram"]
```
